# Optimizing a Trainium2 kernel written in Bass

```python
import numpy as np
import jax
import jax.numpy as jnp

def _softmax(x, axis=-1):
    return jax.nn.softmax(x, axis=axis)

def _gelu(x):
    return jax.nn.gelu(x, approximate=True)

def _silu(x):
    return jax.nn.silu(x)

def _sigmoid(x):
    return jax.nn.sigmoid(x)

def _layernorm(x, axis=-1, eps=1e-05):
    m = jnp.mean(x, axis=axis, keepdims=True)
    v = jnp.var(x, axis=axis, keepdims=True)
    return (x - m) / jnp.sqrt(v + eps)

def _scatter_add(tgt, idx, src, axis=0):
    return tgt.at[idx].add(src)

def _segment_sum(src, seg, n):
    return jax.ops.segment_sum(src, seg, n)
kernel_name = 'mk_xattn_ffn_d1_seqx_r8_aaeb9a'

def setup_inputs(seed: int=0):
    np.random.seed(seed)
    _w = jnp.asarray

    def _rec_inputs():
        import jax
        import jax.numpy as jnp
        _rk = jax.random.key(seed)
        x = -0.0002928 + 1 * jax.random.normal(jax.random.fold_in(_rk, 1), (4, 256, 128), jnp.float32)
        _lenS = 256 - jax.random.randint(jax.random.fold_in(_rk, 7), (4,), 0, max(1, 256 // 4) + 1, jnp.int32)
        _lenS2 = 256 - jax.random.randint(jax.random.fold_in(_rk, 8), (4,), 0, max(1, 256 // 4) + 1, jnp.int32)
        _ctx_1024P = jax.random.normal(jax.random.fold_in(_rk, 11), (4, 16, 128), jnp.float32)
        _ctx_1024c = jax.random.dirichlet(jax.random.fold_in(_rk, 511), 0.3 * jnp.ones((16,), jnp.float32), (4, 256))
        _ctx_1024t = jnp.einsum('bsk,bkd->bsd', _ctx_1024c, _ctx_1024P)
        _ctx_1024t = _ctx_1024t * jax.lax.rsqrt(jnp.mean(jnp.square(_ctx_1024t)) + 1e-12) * 0.953939
        ctx_1024 = -1.39393e-06 + 0.999914 * (_ctx_1024t + 0.3 * jax.random.normal(jax.random.fold_in(_rk, 611), (4, 256, 128), jnp.float32))
        _validS = jnp.arange(256)[None, :] < _lenS[:, None]
        _validS2 = jnp.arange(256)[None, :] < _lenS2[:, None]
        _causal = jnp.tril(jnp.ones((256, 256), dtype=bool))
        mask_BxS2_bf0 = jnp.logical_not(jnp.ones((4, 256), dtype=bool))
        return (x, ctx_1024, mask_BxS2_bf0)
    x, ctx_1024, mask_BxS2_bf0 = _rec_inputs()

    def _L0_xattn_setup():
        import jax, jax.numpy as jnp
        import numpy as np
        EMBED = 128
        HEADS = 16
        HD = EMBED // HEADS
        SCALE_BASE = 64
        OFFSET = 0

        def _dup_interleave(m):
            return jnp.repeat(m, 2, axis=-1)

        def _rotate_every_two(x):
            x1 = x[..., ::2]
            x2 = x[..., 1::2]
            return jnp.stack([-x2, x1], axis=-1).reshape(x.shape)

        def _xpos(x, offset, downscale):
            T = x.shape[2]
            half = HD // 2
            scale_vec = (jnp.arange(0, HD, 2, dtype=jnp.float32) + 0.4 * HD) / (1.4 * HD)
            min_pos = -(T + offset) // 2
            power = jnp.arange(min_pos, min_pos + T, dtype=jnp.float32) / SCALE_BASE
            scale = scale_vec[None, :] ** power[:, None]
            inv_freq = 1.0 / 10000.0 ** (jnp.arange(half, dtype=jnp.float32) / half)
            ang = jnp.arange(T, dtype=jnp.float32)[:, None] * inv_freq[None, :]
            sin, cos = (jnp.sin(ang), jnp.cos(ang))
            if downscale:
                scale = 1.0 / scale
            sin_s = _dup_interleave(sin * scale)
            cos_s = _dup_interleave(cos * scale)
            return x * cos_s + _rotate_every_two(x) * sin_s
        rng = jax.random.key(seed)
        ks = jax.random.split(rng, 8)
        B, T, C = (2, 256, EMBED)
        s = 1.0 / np.sqrt(C)
        return {'query': jax.random.normal(ks[0], (B, T, C), jnp.float32), 'key': jax.random.normal(ks[1], (B, T, C), jnp.float32), 'value': jax.random.normal(ks[2], (B, T, C), jnp.float32), 'key_padding_mask': jnp.zeros((B, T), jnp.bool_), 'Wq': jax.random.normal(ks[3], (C, C), jnp.float32) * s, 'bq': jnp.zeros((C,), jnp.float32), 'Wk': jax.random.normal(ks[4], (C, C), jnp.float32) * s, 'bk': jnp.zeros((C,), jnp.float32), 'Wv': jax.random.normal(ks[5], (C, C), jnp.float32) * s, 'bv': jnp.zeros((C,), jnp.float32), 'Wo': jax.random.normal(ks[6], (C, C), jnp.float32) * s, 'bo': jnp.zeros((C,), jnp.float32)}
    _L0_xattn_all = _L0_xattn_setup()
    _L0_xattn_in = {k: v for k, v in _L0_xattn_all.items() if k in ('Wq', 'bq', 'Wk', 'bk', 'Wv', 'bv', 'Wo', 'bo')}
    del _L0_xattn_all

    def _L0_ffn_setup():
        import jax, jax.numpy as jnp
        import numpy as np
        import math
        D_IN = 128
        FEATURES = (512, 512, 128)
        BATCH, SEQ = (8, 256)

        def _conn_dense(kernel_bool, x):
            w = jnp.where(kernel_bool, jnp.float32(1.0), jnp.float32(-1.0))
            return x @ w
        key = jax.random.key(seed)
        kx, kk0, kk1, kk2 = jax.random.split(key, 4)
        x = jax.random.normal(kx, (BATCH, SEQ, D_IN), dtype=jnp.float32)
        k0 = jax.random.randint(kk0, (2 * D_IN, FEATURES[0]), 0, 2).astype(jnp.bool_)
        k1 = jax.random.randint(kk1, (FEATURES[0], FEATURES[1]), 0, 2).astype(jnp.bool_)
        k2 = jax.random.randint(kk2, (FEATURES[1], FEATURES[2]), 0, 2).astype(jnp.bool_)
        s0 = jnp.asarray(1.0 / math.sqrt(2 * D_IN), dtype=jnp.float32)
        s1 = jnp.asarray(1.0 / math.sqrt(FEATURES[0]), dtype=jnp.float32)
        s2 = jnp.asarray(1.0 / math.sqrt(FEATURES[1]), dtype=jnp.float32)
        return {'x': x, 'k0': k0, 'k1': k1, 'k2': k2, 's0': s0, 's1': s1, 's2': s2}
    _L0_ffn_all = _L0_ffn_setup()
    _L0_ffn_in = {k: v for k, v in _L0_ffn_all.items() if k in ('k0', 'k1', 'k2', 's0', 's1', 's2')}
    del _L0_ffn_all
    return {'x': x, 'ctx_1024': ctx_1024, 'mask_BxS2_bf0': mask_BxS2_bf0, 'L0_xattn_Wq': _L0_xattn_in['Wq'], 'L0_xattn_bq': _L0_xattn_in['bq'], 'L0_xattn_Wk': _L0_xattn_in['Wk'], 'L0_xattn_bk': _L0_xattn_in['bk'], 'L0_xattn_Wv': _L0_xattn_in['Wv'], 'L0_xattn_bv': _L0_xattn_in['bv'], 'L0_xattn_Wo': _L0_xattn_in['Wo'], 'L0_xattn_bo': _L0_xattn_in['bo'], 'L0_ffn_k0': _L0_ffn_in['k0'], 'L0_ffn_k1': _L0_ffn_in['k1'], 'L0_ffn_k2': _L0_ffn_in['k2'], 'L0_ffn_s0': _L0_ffn_in['s0'], 'L0_ffn_s1': _L0_ffn_in['s1'], 'L0_ffn_s2': _L0_ffn_in['s2']}

def reference(x, ctx_1024, mask_BxS2_bf0, L0_xattn_Wq, L0_xattn_bq, L0_xattn_Wk, L0_xattn_bk, L0_xattn_Wv, L0_xattn_bv, L0_xattn_Wo, L0_xattn_bo, L0_ffn_k0, L0_ffn_k1, L0_ffn_k2, L0_ffn_s0, L0_ffn_s1, L0_ffn_s2):
    import jax
    import jax.numpy as jnp

    def _L0_xattn_ref(query, key, value, key_padding_mask, Wq, bq, Wk, bk, Wv, bv, Wo, bo):
        import jax, jax.numpy as jnp
        import numpy as np
        EMBED = 128
        HEADS = 16
        HD = EMBED // HEADS
        SCALE_BASE = 64
        OFFSET = 0

        def _dup_interleave(m):
            return jnp.repeat(m, 2, axis=-1)

        def _rotate_every_two(x):
            x1 = x[..., ::2]
            x2 = x[..., 1::2]
            return jnp.stack([-x2, x1], axis=-1).reshape(x.shape)

        def _xpos(x, offset, downscale):
            T = x.shape[2]
            half = HD // 2
            scale_vec = (jnp.arange(0, HD, 2, dtype=jnp.float32) + 0.4 * HD) / (1.4 * HD)
            min_pos = -(T + offset) // 2
            power = jnp.arange(min_pos, min_pos + T, dtype=jnp.float32) / SCALE_BASE
            scale = scale_vec[None, :] ** power[:, None]
            inv_freq = 1.0 / 10000.0 ** (jnp.arange(half, dtype=jnp.float32) / half)
            ang = jnp.arange(T, dtype=jnp.float32)[:, None] * inv_freq[None, :]
            sin, cos = (jnp.sin(ang), jnp.cos(ang))
            if downscale:
                scale = 1.0 / scale
            sin_s = _dup_interleave(sin * scale)
            cos_s = _dup_interleave(cos * scale)
            return x * cos_s + _rotate_every_two(x) * sin_s
        B, T, C = query.shape

        def split(x):
            return x.reshape(B, T, HEADS, HD).transpose(0, 2, 1, 3)
        q = split(query @ Wq + bq)
        k = split(key @ Wk + bk)
        v = split(value @ Wv + bv)
        k = _xpos(k, 0, True)
        q = _xpos(q, OFFSET, False)
        scores = jnp.einsum('bhtd,bhsd->bhts', q * HD ** (-0.5), k)
        scores = jnp.where(key_padding_mask[:, None, None, :], -jnp.inf, scores)
        probs = jax.nn.softmax(scores.astype(jnp.float32), axis=-1).astype(scores.dtype)
        out = jnp.einsum('bhts,bhsd->bhtd', probs, v)
        out = out.transpose(0, 2, 1, 3).reshape(B, T, C)
        return out @ Wo + bo

    def _L0_ffn_ref(x, k0, k1, k2, s0, s1, s2):
        import jax, jax.numpy as jnp
        import numpy as np
        import math
        D_IN = 128
        FEATURES = (512, 512, 128)
        BATCH, SEQ = (8, 256)

        def _conn_dense(kernel_bool, x):
            w = jnp.where(kernel_bool, jnp.float32(1.0), jnp.float32(-1.0))
            return x @ w
        h = jnp.concatenate([x, -x], axis=-1)
        h = s0 * _conn_dense(k0, h)
        h = jax.nn.relu(h) * 2
        h = s1 * _conn_dense(k1, h)
        h = jax.nn.relu(h) * 2
        h = s2 * _conn_dense(k2, h)
        return h
    x = x + _L0_xattn_ref(_layernorm(x, axis=-1), ctx_1024, ctx_1024, mask_BxS2_bf0, L0_xattn_Wq, L0_xattn_bq, L0_xattn_Wk, L0_xattn_bk, L0_xattn_Wv, L0_xattn_bv, L0_xattn_Wo, L0_xattn_bo)
    x = x + _L0_ffn_ref(_layernorm(x, axis=-1), L0_ffn_k0, L0_ffn_k1, L0_ffn_k2, L0_ffn_s0, L0_ffn_s1, L0_ffn_s2)
    return x

_drawn_inputs = setup_inputs


def setup_inputs(seed=0):
    import zlib

    import numpy as np

    out = dict(_drawn_inputs(seed))
    spreads = {'L0_xattn_bq': (0.0, 0.1),
     'L0_xattn_bk': (0.0, 0.1),
     'L0_xattn_bv': (0.0, 0.1),
     'L0_xattn_bo': (0.0, 0.1)}
    factors = {}
    for name, (base, spread) in spreads.items():
        noise = np.random.default_rng([zlib.crc32(name.encode()), seed]).standard_normal(out[name].shape)
        drawn = base * np.exp(spread * noise) if base else spread * noise
        out[name] = jnp.asarray(drawn.astype(out[name].dtype))
    for name, factor in factors.items():
        out[name] = (out[name] * factor).astype(out[name].dtype)
    return out
```

```python
from contextlib import ExitStack

import concourse.bass as bass
from concourse import mybir
import numpy as np

ALU = mybir.AluOpType
ACT = mybir.ActivationFunctionType
AX = mybir.AxisListType
F32 = mybir.dt.float32
BF16 = mybir.dt.bfloat16
F16 = mybir.dt.float16
U8 = mybir.dt.uint8

P = 128
B, T, C = 4, 256, 128
H, HD = 16, 8
NB = T // P
FH = 512
KC = FH // P
EPS = 1e-5
PARTS = 3
QPART = (0, 1, 2, 0, 1, 0)
KPART = (0, 0, 0, 1, 1, 2)
SLOTS = len(QPART)
SROWS = SLOTS * HD
MASKROW = SROWS
SHIFTROW = SROWS + 1
KMAX = SROWS + 1
KEXP = SROWS + 1 + PARTS
PAIRS = H // 2
G = 4
NG = B * H // G
GPB = H // G
VW = 32

LNS = 2.0 ** 11
S0S = 2.0 ** -4
S1S = 2.0 ** -9
OUTS = 16.0

LAG = 10
PVLAG = 1
S1N, S2N, MN, PN = 2, 2, 3, 8


def program(nc, d):
    heads = B * H
    side = {}

    def at(step, *task):
        side.setdefault(step, []).append(task)

    for b in range(B):
        for kind in "TQKV":
            at(-1, kind, b)
    for b in range(B):
        s = H * (b + 1) + LAG + PVLAG + 1
        last = b == B - 1
        for dt, kind in enumerate(("N1", "N1b", "N2", "N3", "N4", "Fa", "Fb", "Ga", "Gb", "O")):
            step = s + (0, 1, 3, 5, 8, 10, 11, 12, 13, 15)[dt]
            at(step, kind, b)
    for g in range(NG):
        at(G * g + G, "M", g)
    steps = sorted(x for x in side if x >= 0)
    last_step = max(max(steps), heads + LAG + PVLAG + 1)
    order = [t for s in range(-1, last_step + 1) for t in side.get(s, [])]
    slot_of = {t: (n % MN, n // MN) for n, t in enumerate(order)}

    with ExitStack() as ctx:
        def sb(name, shape, dt):
            return ctx.enter_context(nc.sbuf_tensor(name, shape, dt))

        def sem(name):
            return ctx.enter_context(nc.semaphore(name))

        s1 = [ctx.enter_context(nc.psum_tensor(f"s1_{i}", [P, 512], F32)) for i in range(S1N)]
        s2 = [ctx.enter_context(nc.psum_tensor(f"s2_{i}", [P, 512], F32)) for i in range(S2N)]
        pv = ctx.enter_context(nc.psum_tensor("pv", [P, 512], F32))
        misc = [ctx.enter_context(nc.psum_tensor(f"misc{i}", [P, 512], F32)) for i in range(MN)]

        x_sb = sb("x_sb", [P, B, NB, C], F32)
        c_sb = sb("c_sb", [P, B, NB, C], F32)
        wq = sb("wq", [P, 2 * C], F32)
        wk = sb("wk", [P, 2 * C], F32)
        wv = sb("wv", [P, C], F32)
        wo = sb("wo", [P, C], F32)
        ident = sb("ident", [P, P], F32)
        identb = sb("identb", [P, P], BF16)
        rot = sb("rot", [P, 4, T], F32)
        qkbias = sb("qkbias", [P, 4], F32)
        bvb = sb("bvb", [P, C], F32)
        bob = sb("bob", [P, C], F32)
        mask8 = sb("mask8", [1, B * T], U8)
        maskb = sb("maskb", [1, B * T], BF16)
        k0 = sb("k0", [P, 2, FH], U8)
        k1 = sb("k1", [P, KC, FH], U8)
        k2 = sb("k2", [P, KC, C], U8)
        sc = sb("sc", [P, 3], F32)
        sgn = sb("sgn", [P, 8], F32)
        w0d = sb("w0d", [P, 2, FH], F32)
        w0 = sb("w0", [P, FH], F16)
        w1 = sb("w1", [P, KC, FH], F16)
        w2 = sb("w2", [P, KC, C], F16)
        alpha = sb("alpha", [P, 4], F32)
        half = sb("half", [P, NB * B], F32)

        st1 = sb("st1", [P, B * NB, 6], F32)
        mv1 = sb("mv1", [P, B * NB, 2], F32)
        ve1 = sb("ve1", [P, B * NB], F32)
        rs1 = sb("rs1", [P, B * NB], F32)
        xn = sb("xn", [P, B, NB, C], F32)
        xb = sb("xb", [P, B, NB, C], F32)
        xcT = sb("xcT", [P, B, 2, T], F32)
        rca = sb("rca", [P, B, 2, T], F32)
        rcb = sb("rcb", [P, B, 2, T], F32)
        rq, rr = rca, rcb
        parts = sb("parts", [P, B, 2, PARTS, T], BF16)
        qs = sb("qs", [P, B, PAIRS, T], BF16)
        ks = sb("ks", [P, B, PAIRS, T], BF16)
        va = sb("va", [P, B, NB, H, VW], F32)
        pt = sb("pt", [P, PN, NB, T], F32)
        mx = sb("mx", [P, NG, NB, G], F32)
        mr = sb("mr", [P, NG, 2, NB, G], F32)
        mh = sb("mh", [P, NG, NB, G, PARTS], BF16)
        mT = sb("mT", [G * PARTS, NG, T], BF16)
        attU = sb("attU", [P, 2, GPB, T], F32)
        rden = sb("rden", [P, B, NB, H], F32)
        att = sb("att", [P, B, NB, C], F32)
        attT = sb("attT", [P, B, T], F32)
        x1 = sb("x1", [P, B, NB, C], F32)
        st2 = sb("st2", [P, B * NB, 6], F32)
        mv2 = sb("mv2", [P, B * NB, 2], F32)
        ve2 = sb("ve2", [P, B * NB], F32)
        rs2 = sb("rs2", [P, B * NB, 2], F32)
        ln2 = sb("ln2", [P, B, NB, C], F32)
        lnh = sb("lnh", [P, 2, T], F16)
        lnl = sb("lnl", [P, 2, T], F16)
        r1h = sb("r1h", [P, 2, KC, T], F16)
        r1l = sb("r1l", [P, 2, KC, T], F16)
        r2h = sb("r2h", [P, 2, KC, T], F16)
        r2l = sb("r2l", [P, 2, KC, T], F16)
        o_sb = sb("o_sb", [P, B, NB, C], F32)

        x_in = [sem(f"x_in{b}") for b in range(B)]
        c_in = [sem(f"c_in{b}") for b in range(B)]
        ident_in, wqk_in, wv_in, wo_in, rot_in, bias_in, vbias_in, obias_in, ones_in = (
            sem(n) for n in ("ident_in", "wqk_in", "wv_in", "wo_in", "rot_in", "bias_in", "vbias_in", "obias_in",
                             "ones_in"))
        mask_in, s_in, k0_in, k1_in, k2_in = (sem(n) for n in ("mask_in", "s_in", "k0_in", "k1_in", "k2_in"))
        mask_out, maskrow_in = sem("mask_out"), sem("maskrow_in")
        parts_out = [sem(f"parts_out{b}") for b in range(B)]
        stack_in = [sem(f"stack_in{b}") for b in range(B)]
        shift_in = [sem(f"shift_in{g}") for g in range(NG)]
        out_done = sem("out_done")
        misc_full = [sem(f"misc_full{i}") for i in range(MN)]
        names = ("half_set", "va_set", "maskb_done", "stats1", "aggr1", "var1", "rstd1", "xn_done", "xb_done",
                 "xcT_done", "rc_done", "rsum_done", "hi_done", "rem1_done", "mid_done", "lo_done", "va_done",
                 "sgn_step", "w0_step", "w0_done", "w1_done", "w2_done", "alpha_step",
                 "s1_full", "max_done", "m_step", "mparts_done", "mT_done", "s2_full", "exp_done",
                 "pv_full", "attU_done", "rden_done", "att_done", "attT_done", "x1_done", "stats2", "aggr2",
                 "var2", "pow2", "rstd2", "ln2_done", "lnh_done", "lnl_done", "r1h_done", "r1l_done", "r2h_done",
                 "r2l_done", "o_done")
        S = {n: sem(n) for n in names}
        sm = lambda n: S[n]

        block = ctx.enter_context(nc.Block())

        @block.sync
        def _(sp):
            for b in range(B):
                if b == 0:
                    sp.dma_start(x_sb[:, b], d["x"][b].rearrange("(n p) c -> p n c", p=P)).then_inc(x_in[b], 16)
                    sp.dma_start(c_sb[:, b], d["ctx"][b].rearrange("(n p) c -> p n c", p=P)).then_inc(c_in[b], 16)
                    sp.dma_start(wq[:], d["wq"]).then_inc(wqk_in, 16)
                    sp.dma_start(wk[:], d["wk"]).then_inc(wqk_in, 16)
                    sp.dma_start(mask8[:], d["mask"]).then_inc(mask_in, 16)
                else:
                    sp.dma_start(x_sb[:, b], d["x"][b].rearrange("(n p) c -> p n c", p=P)).then_inc(x_in[b], 16)
                    sp.dma_start(c_sb[:, b], d["ctx"][b].rearrange("(n p) c -> p n c", p=P)).then_inc(c_in[b], 16)
            for par in range(2):
                r = 64 * par
                sp.dma_start(qs[r + MASKROW:r + MASKROW + 1, :, :, :], d["ones"][0:1]).then_inc(ones_in, 16)
                sp.dma_start(ks[r + SHIFTROW:r + SHIFTROW + PARTS, :, :, :], d["ones"]).then_inc(ones_in, 16)
            sp.wait_ge(sm("maskb_done"), 1)
            sp.dma_start(d["mask_scr"], maskb[:]).then_inc(mask_out, 16)
            sp.wait_ge(mask_out, 16)
            for par in range(2):
                r = 64 * par + MASKROW
                for b in range(B):
                    sp.dma_start(ks[r:r + 1, b], d["mask_scr"][:, b * T:(b + 1) * T].unsqueeze(1)
                                 .to_broadcast([1, PAIRS, T])).then_inc(maskrow_in, 16)

            def stacks(b):
                scr = d["scr"]
                sp.wait_ge(sm("hi_done"), b + 1)
                sp.dma_start(scr[b, 1, :, 0:3], parts[:, b, 1, 0:1].to_broadcast([P, 3, T])).then_inc(parts_out[b], 16)
                sp.dma_start(scr[b, 0, :, 5:6], parts[:, b, 0, 0:1]).then_inc(parts_out[b], 16)
                sp.wait_ge(sm("mid_done"), b + 1)
                sp.dma_start(scr[b, 1, :, 3:5], parts[:, b, 1, 1:2].to_broadcast([P, 2, T])).then_inc(parts_out[b], 16)
                sp.dma_start(scr[b, 0, :, 3:5], parts[:, b, 0, 0:2]).then_inc(parts_out[b], 16)
                sp.wait_ge(sm("lo_done"), b + 1)
                sp.dma_start(scr[b, 1, :, 5:6], parts[:, b, 1, 2:3]).then_inc(parts_out[b], 16)
                sp.dma_start(scr[b, 0, :, 0:3], parts[:, b, 0, 0:3]).then_inc(parts_out[b], 16)
                sp.wait_ge(parts_out[b], 6 * 16)
                for qk, dst in ((0, qs), (1, ks)):
                    src = scr[b, qk].rearrange("(j two dd) s t -> two (dd s) j t", two=2, dd=HD)
                    for par in range(2):
                        sp.dma_start(dst[64 * par:64 * par + SROWS, b], src[par]).then_inc(stack_in[b], 16)

            def shift(g):
                b, h0 = divmod(G * g, H)
                sp.wait_ge(sm("mT_done"), g + 1)
                for j in range(G):
                    h = h0 + j
                    r = 64 * (h % 2) + SHIFTROW
                    sp.dma_start(qs[r:r + PARTS, b, h // 2], mT[PARTS * j:PARTS * j + PARTS, g]).then_inc(shift_in[g], 16)

            def store(b):
                sp.wait_ge(sm("o_done"), b + 1)
                sp.dma_start(d["out"][b].rearrange("(n p) c -> p n c", p=P), o_sb[:, b]).then_inc(out_done, 16)

            for b in range(B):
                stacks(b)
            for s in range(last_step + 1):
                for t in side.get(s, []):
                    if t[0] == "M":
                        shift(t[1])
                    if t[0] == "O":
                        store(t[1])
            sp.wait_ge(out_done, 16 * B)

        @block.tensor
        def _(pe):
            def claim(task):
                k, use = slot_of[task]
                if use >= 1:
                    kind, b = order[order.index(task) - MN]
                    reader, count = {
                        "T": ("xcT_done", b + 1), "Q": ("rc_done", 4 * b + 2), "K": ("rc_done", 4 * b + 4),
                        "V": ("va_done", NB * (b + 1)), "M": ("mT_done", b + 1),
                        "N1": ("att_done", NB * b + 1), "N1b": ("att_done", NB * b + 2),
                        "N2": ("attT_done", b + 1), "N3": ("x1_done", b + 1), "N4": ("lnl_done", b + 1),
                        "Fa": ("r1l_done", 2 * b + 1), "Fb": ("r1l_done", 2 * b + 2),
                        "Ga": ("r2l_done", 2 * b + 1), "Gb": ("r2l_done", 2 * b + 2), "O": ("o_done", b + 1),
                    }[kind]
                    pe.wait_ge(sm(reader), count)
                return misc[k], misc_full[k]

            def T_(b):
                pe.wait_ge(sm("xn_done"), b + 1)
                pe.wait_ge(c_in[b], 16)
                if b == 0:
                    pe.wait_ge(ident_in, 32)
                ps, full = claim(("T", b))
                for n in range(NB):
                    pe.transpose(ps[:, n * P:(n + 1) * P], xn[:, b, n], ident[:])
                for n in range(NB):
                    mm = pe.transpose(ps[:, T + n * P:T + (n + 1) * P], c_sb[:, b, n], ident[:])
                mm.then_inc(full, 1)

            def QK_(b, kind):
                pe.wait_ge(sm("xcT_done"), b + 1)
                if b == 0 and kind == "Q":
                    pe.wait_ge(wqk_in, 32)
                ps, full = claim((kind, b))
                w, i = (wq, 0) if kind == "Q" else (wk, 1)
                for r in range(2):
                    mm = pe.matmul(ps[:, r * T:(r + 1) * T], w[:, r * C:(r + 1) * C], xcT[:, b, i], start=True, stop=True)
                mm.then_inc(full, 1)

            def V_(b):
                if b == 0:
                    pe.wait_ge(wv_in, 16)
                ps, full = claim(("V", b))
                for n in range(NB):
                    mm = pe.matmul(ps[:, n * C:(n + 1) * C], xcT[:, b, 1, n * P:(n + 1) * P], wv[:], start=True, stop=True)
                mm.then_inc(full, 1)

            def M_(g):
                pe.wait_ge(sm("mparts_done"), g + 1)
                ps, full = claim(("M", g))
                out = ps[:].bitcast(BF16)
                for n in range(NB):
                    mm = pe.transpose(out[0:G * PARTS, n * P:(n + 1) * P], mh[:, g, n].rearrange("p g k -> p (g k)"), identb[:])
                mm.then_inc(full, 1)

            def score_max(i):
                b, h = divmod(i, H)
                r, j = 64 * (h % 2), h // 2
                if h == 0:
                    pe.wait_ge(stack_in[b], 4 * 16)
                if i == 0:
                    pe.wait_ge(ones_in, 64)
                    pe.wait_ge(maskrow_in, 16 * 2 * B)
                if i >= S1N:
                    pe.wait_ge(sm("max_done"), i - S1N + 1)
                for n in range(NB):
                    mm = pe.matmul(s1[i % S1N][:, n * T:(n + 1) * T], qs[r:r + KMAX, b, j, n * P:(n + 1) * P],
                                   ks[r:r + KMAX, b, j, :], start=True, stop=True)
                mm.then_inc(sm("s1_full"), 1)

            def score_exp(i):
                b, h = divmod(i, H)
                r, j = 64 * (h % 2), h // 2
                if i % G == 0:
                    pe.wait_ge(shift_in[i // G], 16 * G)
                if i >= S2N:
                    pe.wait_ge(sm("exp_done"), i - S2N + 1)
                for n in range(NB):
                    mm = pe.matmul(s2[i % S2N][:, n * T:(n + 1) * T], ks[r:r + KEXP, b, j, n * P:(n + 1) * P],
                                   qs[r:r + KEXP, b, j, :], start=True, stop=True)
                mm.then_inc(sm("s2_full"), 1)

            def values(g):
                b, h0 = divmod(G * g, H)
                pe.wait_ge(sm("exp_done"), G * (g + 1))
                pe.wait_ge(sm("va_done"), NB * (b + 1))
                if g >= 1:
                    pe.wait_ge(sm("attU_done"), g)
                for n in range(NB):
                    for j in range(G):
                        mm = pe.matmul(pv[VW * j:VW * (j + 1), 0:T], va[:, b, n, h0 + j],
                                       pt[:, (G * g + j) % PN, n], start=(n == 0), stop=(n == NB - 1))
                mm.then_inc(sm("pv_full"), 1)

            def N1_(b, n):
                pe.wait_ge(sm("attU_done"), GPB * (b + 1))
                ps, full = claim(("N1" if n == 0 else "N1b", b))
                for q in range(GPB):
                    mm = pe.transpose(ps[:, q * P:(q + 1) * P], attU[:, b % 2, q, n * P:(n + 1) * P], ident[:])
                mm.then_inc(full, 1)

            def N2_(b):
                pe.wait_ge(sm("att_done"), NB * (b + 1))
                ps, full = claim(("N2", b))
                for n in range(NB):
                    mm = pe.transpose(ps[:, n * P:(n + 1) * P], att[:, b, n], ident[:])
                mm.then_inc(full, 1)

            def N3_(b):
                pe.wait_ge(sm("attT_done"), b + 1)
                if b == 0:
                    pe.wait_ge(wo_in, 16)
                ps, full = claim(("N3", b))
                for n in range(NB):
                    mm = pe.matmul(ps[:, n * C:(n + 1) * C], attT[:, b, n * P:(n + 1) * P], wo[:], start=True, stop=True)
                mm.then_inc(full, 1)

            def N4_(b):
                pe.wait_ge(sm("ln2_done"), NB * (b + 1))
                ps, full = claim(("N4", b))
                for n in range(NB):
                    mm = pe.transpose(ps[:, n * P:(n + 1) * P], ln2[:, b, n], ident[:])
                mm.then_inc(full, 1)

            def F_(b, f):
                pe.wait_ge(sm("lnl_done"), b + 1)
                if b == 0 and f == 0:
                    pe.wait_ge(sm("w0_done"), 1)
                ps, full = claim(("Fa" if f == 0 else "Fb", b))
                for o in range(2):
                    w = w0[:, (2 * f + o) * P:(2 * f + o + 1) * P]
                    pe.matmul(ps[:, o * T:(o + 1) * T], w, lnh[:, b % 2], start=True, stop=False)
                    mm = pe.matmul(ps[:, o * T:(o + 1) * T], w, lnl[:, b % 2], start=False, stop=True)
                mm.then_inc(full, 1)

            def G_(b, f):
                pe.wait_ge(sm("r1l_done"), 2 * (b + 1))
                if b == 0 and f == 0:
                    pe.wait_ge(sm("w1_done"), 1)
                ps, full = claim(("Ga" if f == 0 else "Gb", b))
                for o in range(2):
                    for k in range(KC):
                        w = w1[:, k, (2 * f + o) * P:(2 * f + o + 1) * P]
                        pe.matmul(ps[:, o * T:(o + 1) * T], w, r1h[:, b % 2, k], start=(k == 0), stop=False)
                        mm = pe.matmul(ps[:, o * T:(o + 1) * T], w, r1l[:, b % 2, k], start=False, stop=(k == KC - 1))
                mm.then_inc(full, 1)

            def O_(b):
                pe.wait_ge(sm("r2l_done"), 2 * (b + 1))
                if b == 0:
                    pe.wait_ge(sm("w2_done"), 1)
                ps, full = claim(("O", b))
                for n in range(NB):
                    for k in range(KC):
                        pe.matmul(ps[:, n * C:(n + 1) * C], r2h[:, b % 2, k, n * P:(n + 1) * P], w2[:, k],
                                  start=(k == 0), stop=False)
                        mm = pe.matmul(ps[:, n * C:(n + 1) * C], r2l[:, b % 2, k, n * P:(n + 1) * P], w2[:, k],
                                       start=False, stop=(k == KC - 1))
                mm.then_inc(full, 1)

            tasks = {"T": T_, "Q": lambda b: QK_(b, "Q"), "K": lambda b: QK_(b, "K"), "V": V_, "M": M_,
                     "N1": lambda b: N1_(b, 0), "N1b": lambda b: N1_(b, 1), "N2": N2_, "N3": N3_, "N4": N4_,
                     "Fa": lambda b: F_(b, 0), "Fb": lambda b: F_(b, 1), "Ga": lambda b: G_(b, 0),
                     "Gb": lambda b: G_(b, 1), "O": O_}
            for kind, b in side.get(-1, []):
                tasks[kind](b)
            for s in range(last_step + 1):
                if s < heads:
                    score_max(s)
                if 0 <= s - LAG < heads:
                    score_exp(s - LAG)
                e = s - LAG - PVLAG
                if 0 <= e < heads and e % G == G - 1:
                    values(e // G)
                for kind, b in side.get(s, []):
                    tasks[kind](b)

        @block.vector
        def _(v):
            def open_(task):
                k, use = slot_of[task]
                v.wait_ge(misc_full[k], use + 1)
                return misc[k]

            def norm1(b):
                v.wait_ge(x_in[b], 16)
                for n in range(NB):
                    v.bn_stats(st1[:, b * NB + n], x_sb[:, b, n]).then_inc(sm("stats1"), 1)
                v.wait_ge(sm("stats1"), NB * (b + 1))
                for n in range(NB):
                    v.bn_aggr(mv1[:, b * NB + n], st1[:, b * NB + n]).then_inc(sm("aggr1"), 1)

            def norm1b(b):
                v.wait_ge(sm("rstd1"), b + 1)
                for n in range(NB):
                    i = b * NB + n
                    ins = v.tensor_scalar(xn[:, b, n], x_sb[:, b, n], mv1[:, i, 0:1], rs1[:, i:i + 1], ALU.subtract, ALU.mult)
                ins.then_inc(sm("xn_done"), 1)

            def rope(b, kind):
                i = 0 if kind == "Q" else 1
                if b == 0 and i == 0:
                    v.wait_ge(rot_in, 16)
                    v.wait_ge(bias_in, 16)
                ps = open_((kind, b))
                v.scalar_tensor_tensor(rca[:, b, i], ps[:, 0:T], qkbias[:, 2 * i:2 * i + 1], rot[:, 2 * i], ALU.add, ALU.mult)\
                    .then_inc(sm("rc_done"), 1)
                v.scalar_tensor_tensor(rcb[:, b, i], ps[:, T:2 * T], qkbias[:, 2 * i + 1:2 * i + 2], rot[:, 2 * i + 1],
                                       ALU.add, ALU.mult).then_inc(sm("rc_done"), 1)

            def split(b):
                v.wait_ge(sm("rc_done"), 4 * (b + 1))
                v.tensor_tensor(rq[:, b], rca[:, b], rcb[:, b], ALU.add).then_inc(sm("rsum_done"), 1)
                v.wait_ge(sm("rsum_done"), b + 1)
                v.tensor_copy(parts[:, b, :, 0], rq[:, b]).then_inc(sm("hi_done"), 1)
                v.wait_ge(sm("hi_done"), b + 1)
                v.tensor_tensor(rr[:, b], rq[:, b], parts[:, b, :, 0], ALU.subtract).then_inc(sm("rem1_done"), 1)
                v.wait_ge(sm("rem1_done"), b + 1)
                v.tensor_copy(parts[:, b, :, 1], rr[:, b]).then_inc(sm("mid_done"), 1)
                v.wait_ge(sm("mid_done"), b + 1)
                v.tensor_tensor(parts[:, b, :, 2], rr[:, b], parts[:, b, :, 1], ALU.subtract).then_inc(sm("lo_done"), 1)

            def V_(b):
                if b == 0:
                    v.wait_ge(vbias_in, 16)
                    v.wait_ge(sm("va_set"), 1)
                ps = open_(("V", b))
                for n in range(NB):
                    ins = v.tensor_tensor(va[:, b, n, :, 0:HD], ps[:, n * C:(n + 1) * C].rearrange("p (h e) -> p h e", h=H),
                                          bvb[:].rearrange("p (h e) -> p h e", h=H), ALU.add)
                    ins.then_inc(sm("va_done"), 1)

            def maximum(i):
                g, j = divmod(i, G)
                v.wait_ge(sm("s1_full"), i + 1)
                v.tensor_reduce(mx[:, g, :, j], s1[i % S1N][:].rearrange("p (n t) -> p n t", n=NB), AX.X, ALU.max)\
                    .then_inc(sm("max_done"), 1)

            def N1_(b, n):
                ps = open_(("N1" if n == 0 else "N1b", b))
                heads_ = ps[:].rearrange("p (h w) -> p h w", w=VW)
                v.reciprocal(rden[:, b, n], heads_[:, :, HD]).then_inc(sm("rden_done"), 1)
                v.wait_ge(sm("rden_done"), NB * b + n + 1)
                v.tensor_tensor(att[:, b, n].rearrange("p (h e) -> p h e", h=H), heads_[:, :, 0:HD],
                                rden[:, b, n].unsqueeze(2).to_broadcast([P, H, HD]), ALU.mult).then_inc(sm("att_done"), 1)

            def N3_(b):
                ps = open_(("N3", b))
                if b == 0:
                    v.wait_ge(sm("xb_done"), 1)
                v.tensor_tensor(x1[:, b].rearrange("p n c -> p (n c)"), ps[:, 0:NB * C], xb[:, b].rearrange("p n c -> p (n c)"),
                                ALU.add).then_inc(sm("x1_done"), 1)
                v.wait_ge(sm("x1_done"), b + 1)
                for n in range(NB):
                    v.bn_stats(st2[:, b * NB + n], x1[:, b, n]).then_inc(sm("stats2"), 1)
                v.wait_ge(sm("stats2"), NB * (b + 1))
                for n in range(NB):
                    v.bn_aggr(mv2[:, b * NB + n], st2[:, b * NB + n]).then_inc(sm("aggr2"), 1)

            def N3b_(b):
                v.wait_ge(sm("rstd2"), b + 1)
                for n in range(NB):
                    i = b * NB + n
                    v.tensor_scalar(ln2[:, b, n], x1[:, b, n], mv2[:, i, 0:1], rs2[:, i, 1:2], ALU.subtract, ALU.mult)\
                        .then_inc(sm("ln2_done"), 1)

            def N4_(b):
                ps = open_(("N4", b))
                v.wait_ge(sm("lnh_done"), b + 1)
                v.tensor_tensor(lnl[:, b % 2], ps[:, 0:T], lnh[:, b % 2], ALU.subtract).then_inc(sm("lnl_done"), 1)

            def relu_lo(b, f, kinds, hi, lo, hi_done, lo_done):
                ps = open_((kinds[f], b))
                v.wait_ge(sm(hi_done), 2 * b + f + 1)
                v.scalar_tensor_tensor(lo[:, b % 2, 2 * f:2 * f + 2].rearrange("p k t -> p (k t)"), ps[:], 0.0,
                                       hi[:, b % 2, 2 * f:2 * f + 2].rearrange("p k t -> p (k t)"), ALU.max, ALU.subtract)\
                    .then_inc(sm(lo_done), 1)

            def O_(b):
                ps = open_(("O", b))
                if b == 0:
                    v.wait_ge(sm("alpha_step"), 3)
                v.scalar_tensor_tensor(o_sb[:, b].rearrange("p n c -> p (n c)"), ps[:, 0:NB * C], alpha[:, 2:3],
                                       x1[:, b].rearrange("p n c -> p (n c)"), ALU.mult, ALU.add).then_inc(sm("o_done"), 1)

            tasks = {"V": V_, "N1": lambda b: N1_(b, 0), "N1b": lambda b: N1_(b, 1), "N3": N3_, "N4": N4_,
                     "Fa": lambda b: relu_lo(b, 0, ("Fa", "Fb"), r1h, r1l, "r1h_done", "r1l_done"),
                     "Fb": lambda b: relu_lo(b, 1, ("Fa", "Fb"), r1h, r1l, "r1h_done", "r1l_done"),
                     "Ga": lambda b: relu_lo(b, 0, ("Ga", "Gb"), r2h, r2l, "r2h_done", "r2l_done"),
                     "Gb": lambda b: relu_lo(b, 1, ("Ga", "Gb"), r2h, r2l, "r2h_done", "r2l_done"), "O": O_}

            for b in range(B):
                norm1(b)
                norm1b(b)
                if b == 0:
                    v.wait_ge(mask_in, 16)
                    v.tensor_scalar(maskb[:], mask8[:], -3.0e38, 3.0e38, ALU.mult, ALU.mult).then_inc(sm("maskb_done"), 1)
            for kind, b in side.get(-1, []):
                if kind in "QK":
                    rope(b, kind)
                if kind == "K":
                    split(b)
                if kind == "V":
                    V_(b)
            for s in range(last_step + 1):
                if s < heads:
                    maximum(s)
                for kind, b in side.get(s, []):
                    if kind in tasks:
                        tasks[kind](b)
                    if kind == "N3":
                        N3b_(b)

        @block.scalar
        def _(a):
            a.dma_start(ident[:], d["ident"]).then_inc(ident_in, 16)
            a.dma_start(rot[:], d["rot"]).then_inc(rot_in, 16)
            a.dma_start(qkbias[:], d["qkbias"]).then_inc(bias_in, 16)
            a.dma_start(wv[:], d["wv"]).then_inc(wv_in, 16)
            a.dma_start(bvb[:], d["bv"]).then_inc(vbias_in, 16)
            a.dma_start(identb[:], d["identb"]).then_inc(ident_in, 16)

            def open_(task):
                k, use = slot_of[task]
                a.wait_ge(misc_full[k], use + 1)
                return misc[k]

            def T_(b):
                ps = open_(("T", b))
                a.copy(xcT[:, b].rearrange("p i t -> p (i t)"), ps[:]).then_inc(sm("xcT_done"), 1)

            def M_(g):
                ps = open_(("M", g))
                a.copy(mT[:, g], ps[:].bitcast(BF16)[0:G * PARTS, 0:T]).then_inc(sm("mT_done"), 1)

            def exponential(i):
                a.wait_ge(sm("s2_full"), i + 1)
                if i >= PN:
                    a.wait_ge(sm("pv_full"), (i - PN) // G + 1)
                a.activation(pt[:, i % PN].rearrange("p n t -> p (n t)"), s2[i % S2N][:], ACT.Exp).then_inc(sm("exp_done"), 1)

            def attU_copy(g):
                b = g // GPB
                if b >= 2 and g % GPB == 0:
                    a.wait_ge(sm("att_done"), NB * (b - 1))
                a.wait_ge(sm("pv_full"), g + 1)
                a.copy(attU[:, b % 2, g % GPB], pv[:, 0:T]).then_inc(sm("attU_done"), 1)

            def N2_(b):
                ps = open_(("N2", b))
                a.copy(attT[:, b], ps[:, 0:T]).then_inc(sm("attT_done"), 1)

            def N4_(b):
                ps = open_(("N4", b))
                if b >= 2:
                    a.wait_ge(sm("r1h_done"), 2 * (b - 1))
                a.copy(lnh[:, b % 2], ps[:, 0:T]).then_inc(sm("lnh_done"), 1)

            def relu_hi(b, f, kinds, hi, hi_done):
                ps = open_((kinds[f], b))
                a.activation(hi[:, b % 2, 2 * f:2 * f + 2].rearrange("p k t -> p (k t)"), ps[:], ACT.Relu)\
                    .then_inc(sm(hi_done), 1)

            tasks = {"M": M_, "N2": N2_, "N4": N4_,
                     "Fa": lambda b: relu_hi(b, 0, ("Fa", "Fb"), r1h, "r1h_done"),
                     "Fb": lambda b: relu_hi(b, 1, ("Fa", "Fb"), r1h, "r1h_done"),
                     "Ga": lambda b: relu_hi(b, 0, ("Ga", "Gb"), r2h, "r2h_done"),
                     "Gb": lambda b: relu_hi(b, 1, ("Ga", "Gb"), r2h, "r2h_done")}
            for kind, b in side.get(-1, []):
                if kind == "T":
                    T_(b)
            for s in range(last_step + 1):
                if 0 <= s - LAG < heads:
                    exponential(s - LAG)
                e = s - LAG - PVLAG
                if 0 <= e < heads and e % G == G - 1:
                    attU_copy(e // G)
                for kind, b in side.get(s, []):
                    if kind in tasks:
                        tasks[kind](b)

        @block.gpsimd
        def _(p):
            p.dma_start(sc[:], d["s"]).then_inc(s_in, 16)
            p.dma_start(k0[:], d["k0"].rearrange("(i p) f -> p i f", p=P)).then_inc(k0_in, 16)
            p.dma_start(k1[:], d["k1"].rearrange("(k p) f -> p k f", p=P)).then_inc(k1_in, 16)
            p.dma_start(k2[:], d["k2"].rearrange("(k p) f -> p k f", p=P)).then_inc(k2_in, 16)
            p.dma_start(wo[:], d["wo"]).then_inc(wo_in, 16)
            p.dma_start(bob[:], d["bo"]).then_inc(obias_in, 16)
            p.memset(half[:], -0.5).then_inc(sm("half_set"), 1)

            def rstd(b, mv, ve, out, aggr, var):
                cols = slice(NB * b, NB * (b + 1))
                p.wait_ge(sm(aggr), NB * (b + 1))
                p.tensor_scalar(ve[:, cols], mv[:, cols, 1], EPS, None, ALU.add).then_inc(sm(var), 1)
                p.wait_ge(sm(var), b + 1)
                return p.tensor_tensor(out, ve[:, cols], half[:, cols], ALU.pow)

            p.wait_ge(sm("half_set"), 1)
            for b in range(B):
                rstd(b, mv1, ve1, rs1[:, NB * b:NB * (b + 1)], "aggr1", "var1").then_inc(sm("rstd1"), 1)
            p.memset(va[:, :, :, :, HD:VW], 1.0).then_inc(sm("va_set"), 1)

            p.wait_ge(s_in, 16)
            n = 0

            def step(ins):
                nonlocal n
                n += 1
                ins.then_inc(sm("w0_step"), 1)
                p.wait_ge(sm("w0_step"), n)

            step(p.tensor_scalar(sgn[:, 0:2], sc[:, 0:2], 0.0, 2.0, ALU.is_ge, ALU.mult))
            step(p.tensor_scalar(sgn[:, 2:4], sgn[:, 0:2], -1.0, None, ALU.add))
            step(p.tensor_tensor(sgn[:, 4:6], sgn[:, 2:4], sc[:, 0:2], ALU.mult))
            step(p.tensor_scalar(sgn[:, 6:7], sgn[:, 3:4], 2 * S1S, None, ALU.mult))
            step(p.tensor_scalar(sgn[:, 7:8], sgn[:, 3:4], -S1S, None, ALU.mult))
            p.tensor_tensor(alpha[:, 0:1], sgn[:, 4:5], sgn[:, 5:6], ALU.mult).then_inc(sm("alpha_step"), 1)
            p.wait_ge(sm("alpha_step"), 1)
            p.tensor_tensor(alpha[:, 1:2], alpha[:, 0:1], sc[:, 2:3], ALU.mult).then_inc(sm("alpha_step"), 1)
            p.wait_ge(sm("alpha_step"), 2)
            p.tensor_scalar(alpha[:, 2:3], alpha[:, 1:2], OUTS, None, ALU.mult).then_inc(sm("alpha_step"), 1)
            p.wait_ge(k0_in, 16)
            step(p.tensor_scalar(w0d[:], k0[:], sgn[:, 2:3], 2 * S0S, ALU.mult, ALU.mult))
            p.tensor_tensor(w0[:], w0d[:, 0], w0d[:, 1], ALU.subtract).then_inc(sm("w0_done"), 1)
            p.wait_ge(obias_in, 16)
            for b in range(B):
                p.wait_ge(x_in[b], 16)
                for n_ in range(NB):
                    ins = p.tensor_tensor(xb[:, b, n_], x_sb[:, b, n_], bob[:], ALU.add)
            ins.then_inc(sm("xb_done"), 1)

            def shift_parts(g):
                p.wait_ge(sm("max_done"), G * (g + 1))
                out = [mh[:, g, :, :, k] for k in range(PARTS)]
                p.tensor_scalar(out[0], mx[:, g], -1.0, None, ALU.mult).then_inc(sm("m_step"), 1)
                p.wait_ge(sm("m_step"), 4 * g + 1)
                p.tensor_tensor(mr[:, g, 0], mx[:, g], out[0], ALU.add).then_inc(sm("m_step"), 1)
                p.wait_ge(sm("m_step"), 4 * g + 2)
                p.tensor_scalar(out[1], mr[:, g, 0], -1.0, None, ALU.mult).then_inc(sm("m_step"), 1)
                p.wait_ge(sm("m_step"), 4 * g + 3)
                p.tensor_tensor(mr[:, g, 1], mr[:, g, 0], out[1], ALU.add).then_inc(sm("m_step"), 1)
                p.wait_ge(sm("m_step"), 4 * g + 4)
                p.tensor_scalar(out[2], mr[:, g, 1], -1.0, None, ALU.mult).then_inc(sm("mparts_done"), 1)

            def N3_(b):
                rstd(b, mv2, ve2, rs2[:, NB * b:NB * (b + 1), 0], "aggr2", "var2").then_inc(sm("pow2"), 1)
                p.wait_ge(sm("pow2"), b + 1)
                p.tensor_scalar(rs2[:, NB * b:NB * (b + 1), 1], rs2[:, NB * b:NB * (b + 1), 0], LNS, None, ALU.mult)\
                    .then_inc(sm("rstd2"), 1)

            def w12(k):
                if k == 0:
                    p.wait_ge(k1_in, 16)
                if k < KC:
                    ins = p.tensor_scalar(w1[:, k], k1[:, k], sgn[:, 6:7], sgn[:, 7:8], ALU.mult, ALU.add)
                    if k == KC - 1:
                        ins.then_inc(sm("w1_done"), 1)
                else:
                    p.wait_ge(k2_in, 16)
                    p.tensor_scalar(w2[:], k2[:], 2.0, -1.0, ALU.mult, ALU.add).then_inc(sm("w2_done"), 1)

            for k in range(KC + 1):
                w12(k)
            for s in range(last_step + 1):
                for kind, b in side.get(s, []):
                    if kind == "M":
                        shift_parts(b)
                    if kind == "N3":
                        N3_(b)


def rotation_tables():
    f = np.float32
    scale_vec = (np.arange(0, HD, 2, dtype=f) + f(0.4 * HD)) / f(1.4 * HD)
    power = np.arange(-T // 2, -T // 2 + T, dtype=f) / f(64)
    scale = (scale_vec[None, :] ** power[:, None]).astype(f)
    inv_freq = (1.0 / f(10000.0) ** (np.arange(HD // 2, dtype=f) / f(HD // 2))).astype(f)
    ang = np.arange(T, dtype=f)[:, None] * inv_freq[None, :]
    sin, cos = np.sin(ang), np.cos(ang)
    sign = np.where(np.arange(HD) % 2 == 0, f(-1), f(1))
    rows = []
    for sc, by in ((scale, f(HD ** -0.5)), (f(1) / scale, f(1))):
        rows.append(np.repeat(cos * sc, 2, axis=1).T * by)
        rows.append(np.repeat(sin * sc, 2, axis=1).T * sign[:, None] * by)
    table = np.stack([np.tile(r, (H, 1)) for r in rows], axis=1)
    return np.ascontiguousarray(table.astype(f))


def kernel(**inputs):
    import concourse.bacc as bacc
    import ml_dtypes
    from concourse.bass_utils import run_bass_kernel_spmd

    g = {k: np.asarray(v) for k, v in inputs.items()}
    swap = np.arange(C).reshape(-1, 2)[:, ::-1].reshape(-1)
    wq, wk, bq, bk = (g[f"L0_xattn_{n}"] for n in ("Wq", "Wk", "bq", "bk"))
    arrays = {
        "x": g["x"], "ctx": g["ctx_1024"], "mask": g["mask_BxS2_bf0"].reshape(1, B * T),
        "wq": np.concatenate([wq, wq[:, swap]], axis=1), "wk": np.concatenate([wk, wk[:, swap]], axis=1),
        "wv": g["L0_xattn_Wv"], "wo": g["L0_xattn_Wo"],
        "qkbias": np.stack([bq, bq[swap], bk, bk[swap]], axis=1),
        "bv": np.broadcast_to(g["L0_xattn_bv"], (P, C)), "bo": np.broadcast_to(g["L0_xattn_bo"], (P, C)),
        "k0": g["L0_ffn_k0"], "k1": g["L0_ffn_k1"], "k2": g["L0_ffn_k2"],
        "s": np.broadcast_to(np.stack([g["L0_ffn_s0"], g["L0_ffn_s1"], g["L0_ffn_s2"]]), (P, 3)),
        "ident": np.eye(P, dtype=np.float32), "identb": np.eye(P).astype(ml_dtypes.bfloat16),
        "ones": np.ones((PARTS, B, PAIRS, T), ml_dtypes.bfloat16), "rot": rotation_tables(),
    }
    arrays = {k: np.ascontiguousarray(v) for k, v in arrays.items()}
    nc = bacc.Bacc("TRN2", target_bir_lowering=False, num_devices=1)
    d = {k: nc.dram_tensor(f"in_{k}", v.shape, mybir.dt.from_np(v.dtype), kind="ExternalInput").ap()
         for k, v in arrays.items()}
    d["scr"] = nc.dram_tensor("scr", (B, 2, P, SLOTS, T), BF16, kind="Internal").ap()
    d["mask_scr"] = nc.dram_tensor("mask_scr", (1, B * T), BF16, kind="Internal").ap()
    d["out"] = nc.dram_tensor("out", (B, T, C), F32, kind="ExternalOutput").ap()
    program(nc, d)
    r = run_bass_kernel_spmd(nc, [{f"in_{k}": v for k, v in arrays.items()}], core_ids=[0])
    return r.results[0]["out"]
```

```python
from contextlib import ExitStack

import concourse.bass as bass
from concourse import mybir
import numpy as np

ALU = mybir.AluOpType
ACT = mybir.ActivationFunctionType
AX = mybir.AxisListType
F32 = mybir.dt.float32
BF16 = mybir.dt.bfloat16
F16 = mybir.dt.float16
U8 = mybir.dt.uint8

P = 128
B, T, C = 4, 256, 128
H, HD = 16, 8
NB = T // P
FH = 512
KC = FH // P
EPS = 1e-5
PARTS = 3
SLOTS = 8
EXTRA = SLOTS - 1
MASKF = PARTS
SROWS = SLOTS * HD
PAIRS = H // 2
G = 4
NG = B * H // G
GPB = H // G
VW = 32

LNS = 2.0 ** 11
S0S = 2.0 ** -4
S1S = 2.0 ** -9
OUTS = 16.0

RINGED = ("T", "Q", "K", "V", "M", "N1", "N1b", "N2", "N3", "N4", "Fa", "Fb", "Ga", "Gb", "O")
POST = [dict(N1=0, N1b=1, N2=3, N3=5, N3x=5, N4=9, Fa=12, Fb=13, Ga=18, Ga2=19, Gb=22, Gb2=23, O=27)] * (B - 1) + \
       [dict(N1=0, N1b=0, N2=2, N3=4, N3x=4, N4=6, Fa=8, Fb=8, Ga=10, Ga2=10, Gb=11, Gb2=11, O=13)]
LATER = {
    "act": dict(N4=1, Fa=1, Fb=1, Ga2=1, Gb2=1, X1=0, X3=0),
    "dve": dict(Q=1, K=1, V=1, N1=1, N1b=1, N3=1, N3x=3, N4=2, Fa=2, Fb=2, Ga2=1, Gb2=1, O=1),
    "pool": dict(N3=2),
}
MLAG = 3
SPLIT1 = 0
PREP2, PREP3 = 2, 9
LOADS = ((0, 2), (0,), (0, 4), (0, 4))
WARM = 10
LAG = 12
PVLAG = 1
S1N, S2N, MN, PN = 2, 2, 3, 8


def program(nc, d):
    heads = B * H
    side = {}

    def at(step, *task):
        side.setdefault(step, []).append(task)

    for b in range(B):
        first = (-1, -1, PREP2, PREP3)[b]
        for kind, dt in dict(T=0, Q=2, K=3, V=4, X0=5, X1=6, X2=7, X3=8, X4=9, Y=11).items():
            at(first if b == 0 or (b == 1 and dt < 5) else dt - 5 + SPLIT1 if b == 1 else first + dt, kind, b)
        for c in range(len(LOADS[b])):
            end = 2 * (LOADS[b] + (PAIRS,))[c + 1]
            at(-1 if b == 0 else SPLIT1 + 7 if b == 1 else H * (b - 2) + end + LAG + 1, "Z", (b, c))
    for b in range(B):
        s = H * (b + 1) + LAG + PVLAG + 1
        for kind, dt in POST[b].items():
            at(s + dt, kind, b)
    at(4, "keep", 0)
    for n, what in enumerate(("w1", "w1", "w1", "w1", "w2", "xb", "xb", "xb", "xb")):
        at(5 + 2 * n, what, min(n, n - 5) if what == "xb" else n)
    for g in range(NG):
        at(G * g + G + MLAG, "M", g)
    steps = sorted(x for x in side if x >= 0)

    def tasks_at(engine, step):
        if step == -1:
            return side[-1]
        return [(kind, b) for s in range(step + 1) for kind, b in side.get(s, [])
                if s + LATER.get(engine, {}).get(kind, 0) == step]
    last_step = max(max(steps) + 3, heads + LAG + PVLAG + 1)
    order = [t for s in range(-1, last_step + 1) for t in side.get(s, []) if t[0] in RINGED]
    slot_of, before, last, used = {}, {}, {}, {}
    for n, t in enumerate(order):
        step = next(s for s in side if t in side[s])
        k = min(range(MN + (S1N if step > heads else 0)), key=lambda k: (last.get(k, -1), k))
        before[t] = order[last[k]] if k in last else "maxima" if k >= MN else None
        slot_of[t] = (k, used.get(k, 0))
        last[k], used[k] = n, used.get(k, 0) + 1

    with ExitStack() as ctx:
        def sb(name, shape, dt):
            return ctx.enter_context(nc.sbuf_tensor(name, shape, dt))

        def sem(name):
            return ctx.enter_context(nc.semaphore(name))

        s1 = [ctx.enter_context(nc.psum_tensor(f"s1_{i}", [P, 512], F32)) for i in range(S1N)]
        s2 = [ctx.enter_context(nc.psum_tensor(f"s2_{i}", [P, 512], F32)) for i in range(S2N)]
        pv = ctx.enter_context(nc.psum_tensor("pv", [P, 512], F32))
        misc = [ctx.enter_context(nc.psum_tensor(f"misc{i}", [P, 512], F32)) for i in range(MN)] + s1

        x_sb = sb("x_sb", [P, B, NB, C], F32)
        c_sb = sb("c_sb", [P, B, NB, C], F32)
        wqk = sb("wqk", [P, 4 * C], F32)
        wq, wk = wqk[:, 0:2 * C], wqk[:, 2 * C:4 * C]
        wvo = sb("wvo", [P, 2 * C], F32)
        wv, wo = wvo[:, 0:C], wvo[:, C:2 * C]
        small = sb("small", [P, 3 * C + 4 + 3], F32)
        ident, bvb, bob = (small[:, i * C:(i + 1) * C] for i in range(3))
        qkbias, sc = small[:, 3 * C:3 * C + 4], small[:, 3 * C + 4:3 * C + 7]
        identb = sb("identb", [P, P], BF16)
        rot = sb("rot", [P, 4, T], F32)
        mask8 = sb("mask8", [B, T], U8)
        maskb = sb("maskb", [B, T], BF16)
        maskT = sb("maskT", [P, B, NB], U8)
        k0 = sb("k0", [P, 2, FH], U8)
        k1 = sb("k1", [P, KC, FH], U8)
        k2 = sb("k2", [P, KC, C], U8)
        sgn = sb("sgn", [P, 8], F32)
        w0d = sb("w0d", [P, 2, FH], F32)
        w0 = sb("w0", [P, FH], F16)
        w1 = sb("w1", [P, KC, FH], F16)
        w2 = sb("w2", [P, KC, C], F16)
        alpha = sb("alpha", [P, 4], F32)
        half = sb("half", [P, NB * B], F32)

        st1 = sb("st1", [P, B * NB, 6], F32)
        mv1 = sb("mv1", [P, B * NB, 2], F32)
        ve1 = sb("ve1", [P, B * NB], F32)
        rs1 = sb("rs1", [P, B * NB], F32)
        xn = sb("xn", [P, B, NB, C], F32)
        xb = sb("xb", [P, B, NB, C], F32)
        xcT = sb("xcT", [P, B, 2, T], F32)
        rca = sb("rca", [P, B, 2, T], F32)
        rcb = sb("rcb", [P, B, 2, T], F32)
        rq, rr = rca, rcb
        parts = sb("parts", [P, B, 2, PARTS, T], BF16)
        warm = sb("warm", [P, 512], BF16)
        qz = sb("qz", [P, 2, H, T], BF16)
        ks = sb("ks", [P, B, PAIRS, T], BF16)
        va = sb("va", [P, B, NB, H, VW], F32)
        pt = sb("pt", [P, PN, NB, T], F32)
        mx = sb("mx", [P, NG, NB, G], F32)
        mr = sb("mr", [P, NG, 2, NB, G], F32)
        mh = sb("mh", [P, NG, NB, G, PARTS], BF16)
        mT = sb("mT", [2 * PARTS, NG, 2, T], BF16)
        attU = sb("attU", [P, 2, GPB, T], F32)
        rden = sb("rden", [P, B, NB, H], F32)
        att = sb("att", [P, B, NB, C], F32)
        attT = sb("attT", [P, B, T], F32)
        x1 = sb("x1", [P, B, NB, C], F32)
        st2 = sb("st2", [P, B * NB, 6], F32)
        mv2 = sb("mv2", [P, B * NB, 2], F32)
        ve2 = sb("ve2", [P, B * NB], F32)
        rs2 = sb("rs2", [P, B * NB], F32)
        ln2 = sb("ln2", [P, B, NB, C], F32)
        lnh = sb("lnh", [P, 2, T], F16)
        lnl = sb("lnl", [P, 2, T], F16)
        r1h = sb("r1h", [P, 2, KC, T], F16)
        r1l = sb("r1l", [P, 2, KC, T], F16)
        r2h = sb("r2h", [P, 2, KC, T], F16)
        r2l = sb("r2l", [P, 2, KC, T], F16)
        o_sb = sb("o_sb", [P, B, NB, C], F32)

        x_first, x_rest, c_first, c_rest = (sem(n) for n in ("x_first", "x_rest", "c_first", "c_rest"))
        x_in = [x_first] + [x_rest] * (B - 1)
        c_in = [c_first] + [c_rest] * (B - 1)
        small_in, identb_in, wqk_in, wvo_in, rot_in = (
            sem(n) for n in ("small_in", "identb_in", "wqk_in", "wvo_in", "rot_in"))
        mask_in, maskT_in, k0_in, k1_in, k2_in = (sem(n) for n in ("mask_in", "maskT_in", "k0_in", "k1_in", "k2_in"))
        extra_out, mask_out, ones_in = sem("extra_out"), sem("mask_out"), sem("ones_in")
        parts_out = [sem(f"parts_out{b}") for b in range(B)]
        stack_in = [[sem(f"stack_in{b}_{c}") for c in range(len(LOADS[b]))] for b in range(B)]
        shift_in = [sem(f"shift_in{g}") for g in range(NG)]
        out_done = sem("out_done")
        misc_full = [sem(f"misc_full{i}") for i in range(MN + S1N)]
        names = ("half_set", "va_set", "keep_done", "warm_set", "qz_even_set", "qz_odd_set", "maskb_done", "stats1", "aggr1", "var1", "rstd1", "xn_done", "xb_done",
                 "xcT_done", "rc_done", "va_done",
                 "sgn_step", "w0_step", "w0_done", "w1_done", "w2_done", "alpha_step",
                 "s1_full", "max_done", "m_step", "mparts_done", "mT_done", "s2_full", "exp_done",
                 "pv_full", "attU_done", "rden_done", "att_done", "attT_done", "x1_done", "stats2", "aggr2",
                 "var2", "pow2", "rstd2", "ln2_done", "lnh_done", "lnl_done", "r1h_done", "r1l_done", "r2h_done",
                 "r2l_done", "o_done")
        S = {n: sem(n) for n in names}
        split_q0, split_k0 = sem("split_q0"), sem("split_k0")
        split_done = [(split_q0, split_k0)] + [(x, x) for x in (sem(f"split{b}") for b in range(1, B))]
        sm = lambda n: S[n]

        block = ctx.enter_context(nc.Block())

        @block.sync
        def _(sp):
            sp.dma_start(x_sb[:, 0], d["x"][0].rearrange("(n p) c -> p n c", p=P)).then_inc(x_first, 16)
            sp.dma_start(wqk[:], d["wqk"]).then_inc(wqk_in, 16)
            tail = "b (n p) c -> p (b n) c"
            sp.dma_start(x_sb[:, 1:].rearrange("p b n c -> p (b n) c"), d["x"][1:].rearrange(tail, p=P)).then_inc(x_rest, 16)
            sp.dma_start(rot[:], d["rot"]).then_inc(rot_in, 16)
            sp.dma_start(mask8[:], d["mask"]).then_inc(mask_in, 16)
            sp.dma_start(d["scr"][:, :, :, EXTRA].rearrange("b i p t -> b (i p) t"),
                         d["extra"].unsqueeze(0).to_broadcast([B, 2 * P, T])).then_inc(extra_out, 16)
            sp.dma_start(wvo[:], d["wvo"]).then_inc(wvo_in, 16)
            sp.dma_start(c_sb[:, 1:].rearrange("p b n c -> p (b n) c"), d["ctx"][1:].rearrange(tail, p=P)).then_inc(c_rest, 16)
            sp.dma_start(identb[:], d["identb"]).then_inc(identb_in, 16)
            sp.dma_start(k0[:], d["k0"].rearrange("(i p) f -> p i f", p=P)).then_inc(k0_in, 16)
            sp.dma_start(maskT[:], d["maskT"]).then_inc(maskT_in, 16)
            sp.wait_ge(sm("maskb_done"), 1)
            sp.wait_ge(extra_out, 16)
            sp.dma_start(d["scr"][:, 1, :, EXTRA].rearrange("b (j e) t -> e b j t", e=2 * HD)[MASKF],
                         maskb[:].unsqueeze(1).to_broadcast([B, PAIRS, T])).then_inc(mask_out, 16)
            sp.wait_ge(sm("qz_odd_set"), 1)
            r = SLOTS * MASKF + EXTRA
            sp.dma_start(qz[r:r + 1].rearrange("p w (j e) t -> p (w j) e t", e=2)[:, :, 1],
                         d["extra"][MASKF:MASKF + 1].unsqueeze(1).to_broadcast([1, 2 * PAIRS, T])).then_inc(ones_in, 16)

            def split_part(i, b, part):
                sp.wait_ge(split_done[b][i], (2, 4, 5)[part])

            def store_parts(b):
                q, k = d["scr"][b, 0], d["scr"][b, 1]
                split_part(1, b, 0)
                sp.dma_start(k[:, 0:3], parts[:, b, 1, 0:1].to_broadcast([P, 3, T])).then_inc(parts_out[b], 16)
                split_part(0, b, 0)
                sp.dma_start(q[:, 6:7], parts[:, b, 0, 0:1]).then_inc(parts_out[b], 16)
                split_part(1, b, 1)
                sp.dma_start(k[:, 3:6], parts[:, b, 1, 1:2].to_broadcast([P, 3, T])).then_inc(parts_out[b], 16)
                split_part(1, b, 2)
                sp.dma_start(k[:, 6:7], parts[:, b, 1, 2:3]).then_inc(parts_out[b], 16)
                split_part(0, b, 2)
                sp.dma_start(q[:, 0:6].rearrange("p (m s) t -> p m (s t)", m=2),
                             parts[:, b, 0].rearrange("p s t -> p (s t)").unsqueeze(1).to_broadcast([P, 2, 3 * T]))\
                    .then_inc(parts_out[b], 16)

            def load_stacks(b, c):
                q, k = d["scr"][b, 0], d["scr"][b, 1]
                js = slice(LOADS[b][c], (LOADS[b] + (PAIRS,))[c + 1])
                if b == 0 and c == 0:
                    sp.wait_ge(mask_out, 16)
                    sp.wait_ge(sm("qz_even_set"), 1)
                    sp.wait_ge(sm("qz_odd_set"), 1)
                sp.wait_ge(parts_out[b], 5 * 16)
                sp.dma_start(ks[:, b, js], k.rearrange("(j e) s t -> (e s) j t", e=2 * HD)[:, js]).then_inc(stack_in[b][c], 16)
                if b >= 2:
                    sp.wait_ge(sm("s2_full"), H * (b - 2) + 2 * js.stop)
                for par in range(2):
                    r = SROWS * par
                    heads_ = slice(2 * js.start + par, 2 * js.stop, 2)
                    sp.dma_start(qz[r:r + SROWS, b % 2, heads_],
                                 q.rearrange("(j two e) s t -> two (e s) j t", two=2, e=HD)[par][:, js])\
                        .then_inc(stack_in[b][c], 16)

            def shift(g):
                b, h0 = divmod(G * g, H)
                sp.wait_ge(sm("mT_done"), g + 1)
                for par in range(2):
                    r = SROWS * par + EXTRA
                    sp.dma_start(qz[r:r + SLOTS * (PARTS - 1) + 1:SLOTS, b % 2, h0 + par:h0 + G:2],
                                 mT[PARTS * par:PARTS * (par + 1), g]).then_inc(shift_in[g], 16)

            def store(b):
                sp.wait_ge(sm("o_done"), b + 1)
                sp.dma_start(d["out"][b].rearrange("(n p) c -> p n c", p=P), o_sb[:, b]).then_inc(out_done, 16)

            for s in range(-1, last_step + 1):
                for t in side.get(s, []):
                    if t[0] == "Y":
                        store_parts(t[1])
                    if t[0] == "Z":
                        load_stacks(*t[1])
                    if t == ("Z", (0, len(LOADS[0]) - 1)):
                        sp.dma_start(k1[:], d["k1"].rearrange("(k p) f -> p k f", p=P)).then_inc(k1_in, 16)
                        sp.dma_start(k2[:], d["k2"].rearrange("(k p) f -> p k f", p=P)).then_inc(k2_in, 16)
                for t in side.get(s, []):
                    if t[0] == "M":
                        shift(t[1])
                    if t[0] == "O":
                        store(t[1])
            sp.wait_ge(out_done, 16 * B)

        def split(eng, b, i, step):
            done = split_done[b][i % 2]
            of = slice(0, 2) if i == 2 else slice(i, i + 1)
            r, rest = rq[:, b, of], rr[:, b, of]
            part = [parts[:, b, of, k] for k in range(PARTS)]
            copy = eng.copy if eng is nc.scalar else eng.tensor_copy if eng is nc.vector else None
            if step == 0:
                eng.wait_ge(sm("rc_done"), 4 * b + (4 if i == 2 else 2 * i + 2))
                ins = eng.tensor_tensor(r, rca[:, b, of], rcb[:, b, of], ALU.add)
            else:
                eng.wait_ge(done, step)
                if step == 1:
                    ins = copy(part[0], r)
                if step == 2:
                    ins = eng.tensor_tensor(rest, r, part[0], ALU.subtract)
                if step == 3:
                    ins = copy(part[1], rest)
                if step == 4:
                    ins = eng.tensor_tensor(part[2], rest, part[1], ALU.subtract)
            ins.then_inc(done, 1)

        @block.tensor
        def _(pe):
            def bank(task):
                k, _ = slot_of[task]
                return misc[k], misc_full[k]

            def claim(task):
                k, _ = slot_of[task]
                if before[task] == "maxima":
                    pe.wait_ge(sm("max_done"), heads)
                elif before[task]:
                    kind, b = before[task]
                    reader, count = {
                        "T": ("xcT_done", b + 1), "Q": ("rc_done", 4 * b + 2), "K": ("rc_done", 4 * b + 4),
                        "V": ("va_done", NB * (b + 1)), "M": ("mT_done", b + 1),
                        "N1": ("att_done", NB * b + 1), "N1b": ("att_done", NB * b + 2),
                        "N2": ("attT_done", b + 1), "N3": ("x1_done", b + 1), "N4": ("lnl_done", b + 1),
                        "Fa": ("r1l_done", 2 * b + 1), "Fb": ("r1l_done", 2 * b + 2),
                        "Ga": ("r2l_done", 2 * b + 1), "Gb": ("r2l_done", 2 * b + 2), "O": ("o_done", b + 1),
                    }[kind]
                    pe.wait_ge(sm(reader), count)
                return misc[k], misc_full[k]

            def T_(b):
                pe.wait_ge(sm("xn_done"), b + 1)
                pe.wait_ge(c_in[b], 16)
                if b == 0:
                    pe.wait_ge(small_in, 16)
                ps, full = claim(("T", b))
                for n in range(NB):
                    pe.transpose(ps[:, n * P:(n + 1) * P], xn[:, b, n], ident[:])
                for n in range(NB):
                    mm = pe.transpose(ps[:, T + n * P:T + (n + 1) * P], c_sb[:, b, n], ident[:])
                mm.then_inc(full, 1)

            def QK_(b, kind):
                pe.wait_ge(sm("xcT_done"), b + 1)
                if b == 0 and kind == "Q":
                    pe.wait_ge(wqk_in, 16)
                ps, full = claim((kind, b))
                w, i = (wq, 0) if kind == "Q" else (wk, 1)
                for r in range(2):
                    mm = pe.matmul(ps[:, r * T:(r + 1) * T], w[:, r * C:(r + 1) * C], xcT[:, b, i], start=True, stop=True)
                mm.then_inc(full, 1)

            def V_(b):
                if b == 0:
                    pe.wait_ge(wvo_in, 16)
                ps, full = claim(("V", b))
                for n in range(NB):
                    mm = pe.matmul(ps[:, n * C:(n + 1) * C], xcT[:, b, 1, n * P:(n + 1) * P], wv[:], start=True, stop=True)
                mm.then_inc(full, 1)

            def M_(g):
                pe.wait_ge(sm("mparts_done"), g + 1)
                ps, full = claim(("M", g))
                out = ps[:].bitcast(BF16)
                if g == 0:
                    pe.wait_ge(identb_in, 16)
                for m in range(2):
                    for n in range(NB):
                        at_ = (m * NB + n) * P
                        mm = pe.transpose(out[0:2 * PARTS, at_:at_ + P],
                                          mh[:, g, n, 2 * m:2 * m + 2].rearrange("p g k -> p (g k)"), identb[:])
                mm.then_inc(full, 1)

            def score_max(i):
                b, h = divmod(i, H)
                if i == 0:
                    pe.wait_ge(ones_in, 16)
                if h % 2 == 0 and h // 2 in LOADS[b]:
                    pe.wait_ge(stack_in[b][LOADS[b].index(h // 2)], 3 * 16)
                if i >= S1N:
                    pe.wait_ge(sm("max_done"), i - S1N + 1)
                for n in range(NB):
                    mm = pe.matmul(s1[i % S1N][:, n * T:(n + 1) * T], qz[:, b % 2, h, n * P:(n + 1) * P],
                                   ks[:, b, h // 2], start=True, stop=True)
                mm.then_inc(sm("s1_full"), 1)

            def score_exp(i):
                b, h = divmod(i, H)
                if i % G == 0:
                    pe.wait_ge(shift_in[i // G], 2 * 16)
                if i >= S2N:
                    pe.wait_ge(sm("exp_done"), i - S2N + 1)
                for n in range(NB):
                    mm = pe.matmul(s2[i % S2N][:, n * T:(n + 1) * T], ks[:, b, h // 2, n * P:(n + 1) * P],
                                   qz[:, b % 2, h], start=True, stop=True)
                mm.then_inc(sm("s2_full"), 1)

            def values(g, n):
                b, h0 = divmod(G * g, H)
                if n == 0:
                    pe.wait_ge(sm("exp_done"), G * (g + 1))
                    pe.wait_ge(sm("va_done"), NB * (b + 1))
                    if g == 0:
                        pe.wait_ge(sm("va_set"), 1)
                        pe.wait_ge(sm("keep_done"), 1)
                    if g >= 1:
                        pe.wait_ge(sm("attU_done"), g)
                for j in range(G):
                    mm = pe.matmul(pv[VW * j:VW * (j + 1), 0:T], va[:, b, n, h0 + j],
                                   pt[:, (G * g + j) % PN, n], start=(n == 0), stop=(n == NB - 1))
                if n == NB - 1:
                    mm.then_inc(sm("pv_full"), 1)

            def N1_(b, n):
                pe.wait_ge(sm("attU_done"), GPB * (b + 1))
                ps, full = claim(("N1" if n == 0 else "N1b", b))
                for q in range(GPB):
                    mm = pe.transpose(ps[:, q * P:(q + 1) * P], attU[:, b % 2, q, n * P:(n + 1) * P], ident[:])
                mm.then_inc(full, 1)

            def N2_(b):
                ps, full = claim(("N2", b))
                for n in range(NB):
                    pe.wait_ge(sm("att_done"), NB * b + n + 1)
                    mm = pe.transpose(ps[:, n * P:(n + 1) * P], att[:, b, n], ident[:])
                mm.then_inc(full, 1)

            def N3_(b):
                pe.wait_ge(sm("attT_done"), b + 1)
                ps, full = claim(("N3", b))
                for n in range(NB):
                    mm = pe.matmul(ps[:, n * C:(n + 1) * C], attT[:, b, n * P:(n + 1) * P], wo[:], start=True, stop=True)
                mm.then_inc(full, 1)

            def N4_(b):
                ps, full = claim(("N4", b))
                for n in range(NB):
                    pe.wait_ge(sm("ln2_done"), NB * b + n + 1)
                    mm = pe.transpose(ps[:, n * P:(n + 1) * P], ln2[:, b, n], ident[:])
                mm.then_inc(full, 1)

            def F_(b, f):
                if b == 0 and f == 0:
                    pe.wait_ge(sm("w0_done"), 1)
                ps, full = claim(("Fa" if f == 0 else "Fb", b))
                for o in range(2):
                    w = w0[:, (2 * f + o) * P:(2 * f + o + 1) * P]
                    for part, done in ((lnh, "lnh_done"), (lnl, "lnl_done")):
                        pe.wait_ge(sm(done), b + 1)
                        mm = pe.matmul(ps[:, o * T:(o + 1) * T], w, part[:, b % 2], start=part is lnh, stop=part is lnl)
                mm.then_inc(full, 1)

            def G_(b, f, o):
                kind = ("Ga", "Gb")[f]
                if b == 0 and f == 0 and o == 0:
                    pe.wait_ge(sm("w1_done"), 1)
                ps, full = claim((kind, b)) if o == 0 else bank((kind, b))
                for part, done in ((r1h, "r1h_done"), (r1l, "r1l_done")):
                    for k in range(KC):
                        pe.wait_ge(sm(done), 2 * b + k // 2 + 1)
                        mm = pe.matmul(ps[:, o * T:(o + 1) * T], w1[:, k, (2 * f + o) * P:(2 * f + o + 1) * P],
                                       part[:, b % 2, k], start=(part is r1h and k == 0),
                                       stop=(part is r1l and k == KC - 1))
                if o == 1:
                    mm.then_inc(full, 1)

            def O_(b):
                if b == 0:
                    pe.wait_ge(sm("w2_done"), 1)
                ps, full = claim(("O", b))
                for n in range(NB):
                    for part, done in ((r2h, "r2h_done"), (r2l, "r2l_done")):
                        for k in range(KC):
                            pe.wait_ge(sm(done), 2 * b + k // 2 + 1)
                            mm = pe.matmul(ps[:, n * C:(n + 1) * C], part[:, b % 2, k, n * P:(n + 1) * P], w2[:, k],
                                           start=(part is r2h and k == 0), stop=(part is r2l and k == KC - 1))
                mm.then_inc(full, 1)

            tasks = {"T": T_, "Q": lambda b: QK_(b, "Q"), "K": lambda b: QK_(b, "K"), "V": V_, "M": M_,
                     "N1": lambda b: N1_(b, 0), "N1b": lambda b: N1_(b, 1), "N2": N2_, "N3": N3_, "N4": N4_,
                     "Fa": lambda b: F_(b, 0), "Fb": lambda b: F_(b, 1), "Ga": lambda b: G_(b, 0, 0),
                     "Ga2": lambda b: G_(b, 0, 1), "Gb": lambda b: G_(b, 1, 0), "Gb2": lambda b: G_(b, 1, 1), "O": O_}
            pe.wait_ge(sm("warm_set"), 1)
            for _ in range(WARM):
                pe.matmul(s1[0][:], warm[:, 0:P], warm[:], start=True, stop=True)
            for kind, b in tasks_at("pe", -1):
                if kind in tasks:
                    tasks[kind](b)
            for s in range(last_step + 1):
                if s < heads:
                    score_max(s)
                if 0 <= s - LAG < heads:
                    score_exp(s - LAG)
                e = s - LAG - PVLAG
                if 0 <= e < heads and e % G == G - 1:
                    values(e // G, 0)
                if 0 <= e - 1 < heads and (e - 1) % G == G - 1:
                    values((e - 1) // G, 1)
                for kind, b in tasks_at("pe", s):
                    if kind in tasks:
                        tasks[kind](b)

        @block.vector
        def _(v):
            def open_(task):
                k, use = slot_of[task]
                v.wait_ge(misc_full[k], use + 1)
                return misc[k]

            def norm1(b):
                v.wait_ge(x_in[b], 16)
                for n in range(NB):
                    v.bn_stats(st1[:, b * NB + n], x_sb[:, b, n]).then_inc(sm("stats1"), 1)
                v.wait_ge(sm("stats1"), NB * (b + 1))
                for n in range(NB):
                    v.bn_aggr(mv1[:, b * NB + n], st1[:, b * NB + n]).then_inc(sm("aggr1"), 1)

            def norm1b(b):
                v.wait_ge(sm("rstd1"), b + 1)
                for n in range(NB):
                    i = b * NB + n
                    ins = v.tensor_scalar(xn[:, b, n], x_sb[:, b, n], mv1[:, i, 0:1], rs1[:, i:i + 1], ALU.subtract, ALU.mult)
                ins.then_inc(sm("xn_done"), 1)

            def rope(b, kind):
                i = 0 if kind == "Q" else 1
                if b == 0 and i == 0:
                    v.wait_ge(rot_in, 16)
                    v.wait_ge(small_in, 16)
                ps = open_((kind, b))
                v.scalar_tensor_tensor(rca[:, b, i], ps[:, 0:T], qkbias[:, 2 * i:2 * i + 1], rot[:, 2 * i], ALU.add, ALU.mult)\
                    .then_inc(sm("rc_done"), 1)
                v.scalar_tensor_tensor(rcb[:, b, i], ps[:, T:2 * T], qkbias[:, 2 * i + 1:2 * i + 2], rot[:, 2 * i + 1],
                                       ALU.add, ALU.mult).then_inc(sm("rc_done"), 1)

            def V_(b):
                ps = open_(("V", b))
                for n in range(NB):
                    ins = v.tensor_tensor(va[:, b, n, :, 0:HD], ps[:, n * C:(n + 1) * C].rearrange("p (h e) -> p h e", h=H),
                                          bvb[:].rearrange("p (h e) -> p h e", h=H), ALU.add)
                    ins.then_inc(sm("va_done"), 1)

            def maximum(i):
                g, j = divmod(i, G)
                v.wait_ge(sm("s1_full"), i + 1)
                v.tensor_reduce(mx[:, g, :, j], s1[i % S1N][:].rearrange("p (n t) -> p n t", n=NB), AX.X, ALU.max)\
                    .then_inc(sm("max_done"), 1)

            def N1_(b, n):
                ps = open_(("N1" if n == 0 else "N1b", b))
                heads_ = ps[:].rearrange("p (h w) -> p h w", w=VW)
                v.reciprocal(rden[:, b, n], heads_[:, :, HD]).then_inc(sm("rden_done"), 1)
                v.wait_ge(sm("rden_done"), NB * b + n + 1)
                v.tensor_tensor(att[:, b, n].rearrange("p (h e) -> p h e", h=H), heads_[:, :, 0:HD],
                                rden[:, b, n].unsqueeze(2).to_broadcast([P, H, HD]), ALU.mult).then_inc(sm("att_done"), 1)

            def N3_(b):
                ps = open_(("N3", b))
                v.wait_ge(sm("xb_done"), b + 1)
                v.tensor_tensor(x1[:, b].rearrange("p n c -> p (n c)"), ps[:, 0:NB * C], xb[:, b].rearrange("p n c -> p (n c)"),
                                ALU.add).then_inc(sm("x1_done"), 1)
                v.wait_ge(sm("x1_done"), b + 1)
                for n in range(NB):
                    v.bn_stats(st2[:, b * NB + n], x1[:, b, n]).then_inc(sm("stats2"), 1)
                v.wait_ge(sm("stats2"), NB * (b + 1))
                for n in range(NB):
                    v.bn_aggr(mv2[:, b * NB + n], st2[:, b * NB + n]).then_inc(sm("aggr2"), 1)

            def N3b_(b):
                v.wait_ge(sm("rstd2"), b + 1)
                for n in range(NB):
                    i = b * NB + n
                    v.tensor_scalar(ln2[:, b, n], x1[:, b, n], mv2[:, i, 0:1], rs2[:, i:i + 1], ALU.subtract, ALU.mult)\
                        .then_inc(sm("ln2_done"), 1)

            def N4_(b):
                ps = open_(("N4", b))
                v.wait_ge(sm("lnh_done"), b + 1)
                v.scalar_tensor_tensor(lnl[:, b % 2], ps[:, 0:T], LNS, lnh[:, b % 2], ALU.mult, ALU.subtract).then_inc(sm("lnl_done"), 1)

            def relu_lo(b, f, kinds, hi, lo, hi_done, lo_done):
                ps = open_((kinds[f], b))
                v.wait_ge(sm(hi_done), 2 * b + f + 1)
                v.scalar_tensor_tensor(lo[:, b % 2, 2 * f:2 * f + 2].rearrange("p k t -> p (k t)"), ps[:], 0.0,
                                       hi[:, b % 2, 2 * f:2 * f + 2].rearrange("p k t -> p (k t)"), ALU.max, ALU.subtract)\
                    .then_inc(sm(lo_done), 1)

            def O_(b):
                ps = open_(("O", b))
                if b == 0:
                    v.wait_ge(sm("alpha_step"), 3)
                v.scalar_tensor_tensor(o_sb[:, b].rearrange("p n c -> p (n c)"), ps[:, 0:NB * C], alpha[:, 2:3],
                                       x1[:, b].rearrange("p n c -> p (n c)"), ALU.mult, ALU.add).then_inc(sm("o_done"), 1)

            tasks = {"Q": lambda b: rope(b, "Q"), "K": lambda b: rope(b, "K"), "V": V_,
                     "N1": lambda b: N1_(b, 0), "N1b": lambda b: N1_(b, 1), "N3": N3_, "N3x": N3b_, "N4": N4_,
                     "Fa": lambda b: relu_lo(b, 0, ("Fa", "Fb"), r1h, r1l, "r1h_done", "r1l_done"),
                     "Fb": lambda b: relu_lo(b, 1, ("Fa", "Fb"), r1h, r1l, "r1h_done", "r1l_done"),
                     "Ga2": lambda b: relu_lo(b, 0, ("Ga", "Gb"), r2h, r2l, "r2h_done", "r2l_done"),
                     "Gb2": lambda b: relu_lo(b, 1, ("Ga", "Gb"), r2h, r2l, "r2h_done", "r2l_done"), "O": O_}

            v.memset(qz[SROWS:P, :, 0::2, :].bitcast(mybir.dt.uint32), 0).then_inc(sm("qz_even_set"), 1)
            norm1(0)
            norm1b(0)
            v.wait_ge(mask_in, 16)
            v.tensor_scalar(maskb[:], mask8[:], -3.0e38, None, ALU.mult).then_inc(sm("maskb_done"), 1)
            norm1(1)
            rope(0, "Q")
            rope(0, "K")
            for step in range(5):
                split(nc.vector, 0, 1, step)
            norm1b(1)
            V_(0)
            norm1(2)
            norm1(3)
            norm1b(2)
            norm1b(3)
            rope(1, "Q")
            rope(1, "K")
            V_(1)
            for s in range(last_step + 1):
                if s < heads:
                    maximum(s)
                for kind, b in tasks_at("dve", s):
                    if kind in tasks:
                        tasks[kind](b)

        @block.scalar
        def _(a):
            a.dma_start(small[:], d["small"]).then_inc(small_in, 16)
            a.dma_start(c_sb[:, 0], d["ctx"][0].rearrange("(n p) c -> p n c", p=P)).then_inc(c_first, 16)

            def open_(task):
                k, use = slot_of[task]
                a.wait_ge(misc_full[k], use + 1)
                return misc[k]

            def T_(b):
                ps = open_(("T", b))
                a.copy(xcT[:, b].rearrange("p i t -> p (i t)"), ps[:]).then_inc(sm("xcT_done"), 1)

            def M_(g):
                ps = open_(("M", g))
                a.copy(mT[:, g].rearrange("p m t -> p (m t)"), ps[:].bitcast(BF16)[0:2 * PARTS, 0:2 * T]).then_inc(sm("mT_done"), 1)

            def exponential(i):
                a.wait_ge(sm("s2_full"), i + 1)
                if i >= PN:
                    a.wait_ge(sm("pv_full"), (i - PN) // G + 1)
                a.activation(pt[:, i % PN].rearrange("p n t -> p (n t)"), s2[i % S2N][:], ACT.Exp).then_inc(sm("exp_done"), 1)

            def attU_copy(g):
                b = g // GPB
                if b >= 2 and g % GPB == 0:
                    a.wait_ge(sm("att_done"), NB * (b - 1))
                a.wait_ge(sm("pv_full"), g + 1)
                a.copy(attU[:, b % 2, g % GPB], pv[:, 0:T]).then_inc(sm("attU_done"), 1)

            def N2_(b):
                ps = open_(("N2", b))
                a.copy(attT[:, b], ps[:, 0:T]).then_inc(sm("attT_done"), 1)

            def N4_(b):
                ps = open_(("N4", b))
                if b >= 2:
                    a.wait_ge(sm("r1h_done"), 2 * (b - 1))
                a.activation(lnh[:, b % 2], ps[:, 0:T], ACT.Copy, scale=LNS).then_inc(sm("lnh_done"), 1)

            def relu_hi(b, f, kinds, hi, hi_done):
                ps = open_((kinds[f], b))
                a.activation(hi[:, b % 2, 2 * f:2 * f + 2].rearrange("p k t -> p (k t)"), ps[:], ACT.Relu)\
                    .then_inc(sm(hi_done), 1)

            tasks = {"X1": lambda b: split(nc.scalar, b, 2, 1), "X3": lambda b: split(nc.scalar, b, 2, 3), "T": T_, "M": M_, "N2": N2_, "N4": N4_,
                     "Fa": lambda b: relu_hi(b, 0, ("Fa", "Fb"), r1h, "r1h_done"),
                     "Fb": lambda b: relu_hi(b, 1, ("Fa", "Fb"), r1h, "r1h_done"),
                     "Ga2": lambda b: relu_hi(b, 0, ("Ga", "Gb"), r2h, "r2h_done"),
                     "Gb2": lambda b: relu_hi(b, 1, ("Ga", "Gb"), r2h, "r2h_done")}
            T_(0)
            split(nc.scalar, 0, 0, 1)
            split(nc.scalar, 0, 0, 3)
            T_(1)
            for s in range(last_step + 1):
                if 0 <= s - LAG < heads:
                    exponential(s - LAG)
                e = s - LAG - PVLAG - 1
                if 0 <= e < heads and e % G == G - 1:
                    attU_copy(e // G)
                for kind, b in tasks_at("act", s):
                    if kind in tasks:
                        tasks[kind](b)

        @block.gpsimd
        def _(p):
            p.memset(warm[:], 0.0).then_inc(sm("warm_set"), 1)
            p.memset(half[:], -0.5).then_inc(sm("half_set"), 1)
            p.memset(qz[0:SROWS, :, 1::2, :].bitcast(mybir.dt.uint32), 0).then_inc(sm("qz_odd_set"), 1)

            def rstd(b, mv, ve, out, aggr, var):
                cols = slice(NB * b, NB * (b + 1))
                p.wait_ge(sm(aggr), NB * (b + 1))
                p.tensor_scalar(ve[:, cols], mv[:, cols, 1], EPS, None, ALU.add).then_inc(sm(var), 1)
                p.wait_ge(sm(var), b + 1)
                return p.tensor_tensor(out, ve[:, cols], half[:, cols], ALU.pow)

            p.wait_ge(sm("half_set"), 1)
            def norm1(b):
                rstd(b, mv1, ve1, rs1[:, NB * b:NB * (b + 1)], "aggr1", "var1").then_inc(sm("rstd1"), 1)

            norm1(0)
            p.memset(va[:, :, :, :, HD + 1:VW], 0.0).then_inc(sm("va_set"), 1)
            norm1(1)
            split(nc.gpsimd, 0, 0, 0)
            split(nc.gpsimd, 0, 0, 2)
            split(nc.gpsimd, 0, 0, 4)
            norm1(2)
            norm1(3)
            p.wait_ge(small_in, 16)
            n = 0

            def step(ins):
                nonlocal n
                n += 1
                ins.then_inc(sm("w0_step"), 1)
                p.wait_ge(sm("w0_step"), n)

            step(p.tensor_scalar(sgn[:, 0:2], sc[:, 0:2], 0.0, 2.0, ALU.is_ge, ALU.mult))
            step(p.tensor_scalar(sgn[:, 2:4], sgn[:, 0:2], -1.0, None, ALU.add))
            step(p.tensor_tensor(sgn[:, 4:6], sgn[:, 2:4], sc[:, 0:2], ALU.mult))
            step(p.tensor_scalar(sgn[:, 6:7], sgn[:, 3:4], 2 * S1S, None, ALU.mult))
            step(p.tensor_scalar(sgn[:, 7:8], sgn[:, 3:4], -S1S, None, ALU.mult))
            p.tensor_tensor(alpha[:, 0:1], sgn[:, 4:5], sgn[:, 5:6], ALU.mult).then_inc(sm("alpha_step"), 1)
            p.wait_ge(sm("alpha_step"), 1)
            p.tensor_tensor(alpha[:, 1:2], alpha[:, 0:1], sc[:, 2:3], ALU.mult).then_inc(sm("alpha_step"), 1)
            p.wait_ge(sm("alpha_step"), 2)
            p.tensor_scalar(alpha[:, 2:3], alpha[:, 1:2], OUTS, None, ALU.mult).then_inc(sm("alpha_step"), 1)
            p.wait_ge(k0_in, 16)
            step(p.tensor_scalar(w0d[:], k0[:], sgn[:, 2:3], 2 * S0S, ALU.mult, ALU.mult))
            p.tensor_tensor(w0[:], w0d[:, 0], w0d[:, 1], ALU.subtract).then_inc(sm("w0_done"), 1)

            def xb_(b):
                p.wait_ge(x_in[b], 16)
                for n_ in range(NB):
                    ins = p.tensor_tensor(xb[:, b, n_], x_sb[:, b, n_], bob[:], ALU.add)
                ins.then_inc(sm("xb_done"), 1)

            def shift_parts(g):
                p.wait_ge(sm("max_done"), G * (g + 1))
                out = [mh[:, g, :, :, k] for k in range(PARTS)]
                p.tensor_scalar(out[0], mx[:, g], -1.0, None, ALU.mult).then_inc(sm("m_step"), 1)
                p.wait_ge(sm("m_step"), 4 * g + 1)
                p.tensor_tensor(mr[:, g, 0], mx[:, g], out[0], ALU.add).then_inc(sm("m_step"), 1)
                p.wait_ge(sm("m_step"), 4 * g + 2)
                p.tensor_scalar(out[1], mr[:, g, 0], -1.0, None, ALU.mult).then_inc(sm("m_step"), 1)
                p.wait_ge(sm("m_step"), 4 * g + 3)
                p.tensor_tensor(mr[:, g, 1], mr[:, g, 0], out[1], ALU.add).then_inc(sm("m_step"), 1)
                p.wait_ge(sm("m_step"), 4 * g + 4)
                p.tensor_scalar(out[2], mr[:, g, 1], -1.0, None, ALU.mult).then_inc(sm("mparts_done"), 1)

            def keep_column():
                p.wait_ge(maskT_in, 16)
                p.tensor_scalar(va[:, :, :, :, HD].rearrange("p b n h -> p (b n) h"),
                                maskT[:].rearrange("p b n -> p (b n)").unsqueeze(2).to_broadcast([P, B * NB, H]),
                                -1.0, 1.0, ALU.mult, ALU.add).then_inc(sm("keep_done"), 1)

            def N3_(b):
                cols = slice(b * NB, (b + 1) * NB)
                p.wait_ge(sm("aggr2"), NB * (b + 1))
                rstd(b, mv2, ve2, rs2[:, cols], "aggr2", "var2").then_inc(sm("rstd2"), 1)

            def w12(k):
                if k == 0:
                    p.wait_ge(k1_in, 16)
                if k < KC:
                    ins = p.tensor_scalar(w1[:, k], k1[:, k], sgn[:, 6:7], sgn[:, 7:8], ALU.mult, ALU.add)
                    if k == KC - 1:
                        ins.then_inc(sm("w1_done"), 1)
                else:
                    p.wait_ge(k2_in, 16)
                    p.tensor_scalar(w2[:], k2[:], 2.0, -1.0, ALU.mult, ALU.add).then_inc(sm("w2_done"), 1)

            for s in range(last_step + 1):
                if s % G == G - 1 and s < heads:
                    shift_parts(s // G)
                for kind, b in tasks_at("pool", s):
                    if kind in ("X0", "X2", "X4"):
                        split(nc.gpsimd, b, 2, int(kind[1]))
                    if kind == "keep":
                        keep_column()
                    if kind in ("w1", "w2"):
                        w12(b)
                    if kind == "xb":
                        xb_(b)
                    if kind == "N3":
                        N3_(b)


def rotation_tables():
    f = np.float32
    scale_vec = (np.arange(0, HD, 2, dtype=f) + f(0.4 * HD)) / f(1.4 * HD)
    power = np.arange(-T // 2, -T // 2 + T, dtype=f) / f(64)
    scale = (scale_vec[None, :] ** power[:, None]).astype(f)
    inv_freq = (1.0 / f(10000.0) ** (np.arange(HD // 2, dtype=f) / f(HD // 2))).astype(f)
    ang = np.arange(T, dtype=f)[:, None] * inv_freq[None, :]
    sin, cos = np.sin(ang), np.cos(ang)
    sign = np.where(np.arange(HD) % 2 == 0, f(-1), f(1))
    rows = []
    for sc, by in ((scale, f(HD ** -0.5)), (f(1) / scale, f(1))):
        rows.append(np.repeat(cos * sc, 2, axis=1).T * by)
        rows.append(np.repeat(sin * sc, 2, axis=1).T * sign[:, None] * by)
    table = np.stack([np.tile(r, (H, 1)) for r in rows], axis=1)
    return np.ascontiguousarray(table.astype(f))


def kernel(**inputs):
    import concourse.bacc as bacc
    import ml_dtypes
    from concourse.bass_utils import run_bass_kernel_spmd

    g = {k: np.asarray(v) for k, v in inputs.items()}
    swap = np.arange(C).reshape(-1, 2)[:, ::-1].reshape(-1)
    wq, wk, bq, bk = (g[f"L0_xattn_{n}"] for n in ("Wq", "Wk", "bq", "bk"))
    extra = np.zeros((2, H, HD, T), np.float32)
    extra[0, :, MASKF] = 1
    extra[1, :, :PARTS] = 1
    extra = extra.reshape(2 * P, T)
    arrays = {
        "x": g["x"], "ctx": g["ctx_1024"], "mask": g["mask_BxS2_bf0"],
        "maskT": g["mask_BxS2_bf0"].reshape(B, NB, P).transpose(2, 0, 1),
        "wqk": np.concatenate([wq, wq[:, swap], wk, wk[:, swap]], axis=1),
        "wvo": np.concatenate([g["L0_xattn_Wv"], g["L0_xattn_Wo"]], axis=1),
        "small": np.concatenate([
            np.eye(P, dtype=np.float32), np.broadcast_to(g["L0_xattn_bv"], (P, C)),
            np.broadcast_to(g["L0_xattn_bo"], (P, C)), np.stack([bq, bq[swap], bk, bk[swap]], axis=1),
            np.broadcast_to(np.stack([g["L0_ffn_s0"], g["L0_ffn_s1"], g["L0_ffn_s2"]]), (P, 3))], axis=1),
        "k0": g["L0_ffn_k0"], "k1": g["L0_ffn_k1"], "k2": g["L0_ffn_k2"],
        "identb": np.eye(P).astype(ml_dtypes.bfloat16), "extra": extra.astype(ml_dtypes.bfloat16),
        "rot": rotation_tables(),
    }
    arrays = {k: np.ascontiguousarray(v) for k, v in arrays.items()}
    nc = bacc.Bacc("TRN2", target_bir_lowering=False, num_devices=1)
    d = {k: nc.dram_tensor(f"in_{k}", v.shape, mybir.dt.from_np(v.dtype), kind="ExternalInput").ap()
         for k, v in arrays.items()}
    d["scr"] = nc.dram_tensor("scr", (B, 2, P, SLOTS, T), BF16, kind="Internal").ap()
    d["mask_scr"] = nc.dram_tensor("mask_scr", (1, B * T), BF16, kind="Internal").ap()
    d["out"] = nc.dram_tensor("out", (B, T, C), F32, kind="ExternalOutput").ap()
    program(nc, d)
    r = run_bass_kernel_spmd(nc, [{f"in_{k}": v for k, v in arrays.items()}], core_ids=[0])
    return r.results[0]["out"]
```

```python
from contextlib import ExitStack

import concourse.bass as bass
from concourse import mybir
import numpy as np

ALU = mybir.AluOpType
ACT = mybir.ActivationFunctionType
AX = mybir.AxisListType
F32 = mybir.dt.float32
BF16 = mybir.dt.bfloat16
F16 = mybir.dt.float16
U8 = mybir.dt.uint8

P = 128
B, T, C = 4, 256, 128
H, HD = 16, 8
NB = T // P
FH = 512
KC = FH // P
EPS = 1e-5
PARTS = 3
SLOTS = 8
EXTRA = SLOTS - 1
MASKF = PARTS
SROWS = SLOTS * HD
PAIRS = H // 2
QPART, KPART = (0, 1, 2, 0, 1, 2, 0), (0, 0, 0, 1, 1, 1, 2)
G = 4
NG = B * H // G
GPB = H // G
VW = 32

LNS = 2.0 ** 11
S0S = 2.0 ** -4
S1S = 2.0 ** -9
OUTS = 16.0

RINGED = ("T", "Q", "K", "V", "M", "N1", "N1b", "N2", "N3", "N4", "Fa", "Fb", "Ga", "Gb", "O")
POST = (
    dict(N1=0, N1b=1, N2=3, N3=5, N3x=5, N4=9, Fa=12, Fb=13, Ga=18, Ga2=19, Gb=22, Gb2=24, O=26),
    dict(N1=0, N1b=1, N2=4, N3=5, N3x=5, N4=9, Fa=11, Fb=14, Ga=18, Ga2=19, Gb=21, Gb2=25, O=28),
    dict(N1=1, N1b=1, N2=3, N3=5, N3x=5, N4=9, Fa=12, Fb=12, Ga=18, Ga2=21, Gb=22, Gb2=23, O=28),
    dict(N1=0, N1b=0, N2=2, N3=4, N3x=4, N4=6, Fa=7, Fb=7, Ga=9, Ga2=10, Gb=10, Gb2=10, O=12),
)
LATER = {
    "act": dict(V=0, N4=1, Fa=1, Fb=1, Ga2=0, Gb2=0, X1=0, X3=0),
    "dve": dict(Q=0, K=1, V=2, N1=1, N1b=1, N3=1, N3x=3, N4=1, Fa=2, Fb=2, Ga2=1, Gb2=1, O=1),
    "pool": dict(N3=3),
}
MLAG = 2
PREP = (
    dict(L=-1, Lx=-1, T=-1, Q=-1, K=-1, V=-1, X0=-1, X1=-1, X2=-1, X3=-1, X4=-1, Y=-1),
    dict(L=-1, Lx=-1, T=0, Q=1, K=0, V=1, X0=1, X1=2, X2=4, X3=7, X4=7, Y=7),
    dict(L=0, Lx=3, T=5, Q=7, K=8, V=9, X0=10, X1=11, X2=12, X3=13, X4=13, Y=13),
    dict(L=7, Lx=9, T=11, Q=13, K=14, V=15, X0=16, X1=17, X2=18, X3=19, X4=20, Y=22),
)
WSTEPS = (5, 7, 9, 12, 13, 15, 17, 21, 23)
Z1 = 13
FIRST = 2
LOADS = ((2, 4), (0,), (0, 3, 7), (0, 4))
WARM = 10
WARM2 = 6
LAG0, GROW, LAG = 11, 4, 14
PVLAG = 2
NSEL = FIRST * PARTS * 3 + 2
S1N, S2N, MN, PN = 2, 2, 3, 8


def program(nc, d):
    heads = B * H
    exp_step = [i + min(LAG, LAG0 + i // GROW) for i in range(heads)]
    exp_at = {s: i for i, s in enumerate(exp_step)}
    side = {}

    def at(step, *task):
        side.setdefault(step, []).append(task)

    for b in range(B):
        for kind, step in PREP[b].items():
            at(step, kind, b)
        for c in range(len(LOADS[b])):
            end = 2 * (LOADS[b] + (PAIRS,))[c + 1]
            at(-1 if b == 0 else Z1 if b == 1 else exp_step[H * (b - 2) + end - 1] + 2, "Z", (b, c))
    for b in range(B):
        s = exp_step[H * (b + 1) - 1] + PVLAG + 2
        for kind, dt in POST[b].items():
            at(s + dt, kind, b)
    at(4, "keep", 0)
    for n, what in enumerate(("w1", "w1", "w1", "w1", "w2", "xb", "xb", "xb", "xb")):
        at(WSTEPS[n], what, min(n, n - 5) if what == "xb" else n)
    for g in range(NG):
        at(G * g + G + MLAG, "M", g)
    steps = sorted(x for x in side if x >= 0)

    def tasks_at(engine, step):
        if step == -1:
            return side[-1]
        return [(kind, b) for s in range(step + 1) for kind, b in side.get(s, [])
                if s + LATER.get(engine, {}).get(kind, 0) == step]
    last_step = max(max(steps) + 3, exp_step[-1] + PVLAG + 2)
    order = [t for s in range(-1, last_step + 1) for t in side.get(s, []) if t[0] in RINGED]
    slot_of, before, last, used = {}, {}, {}, {}
    for n, t in enumerate(order):
        step = next(s for s in side if t in side[s])
        k = min(range(MN + (S1N if step > heads else 0)), key=lambda k: (last.get(k, -1), k))
        before[t] = order[last[k]] if k in last else "maxima" if k >= MN else None
        slot_of[t] = (k, used.get(k, 0))
        last[k], used[k] = n, used.get(k, 0) + 1

    with ExitStack() as ctx:
        def sb(name, shape, dt):
            return ctx.enter_context(nc.sbuf_tensor(name, shape, dt))

        def sem(name):
            return ctx.enter_context(nc.semaphore(name))

        s1 = [ctx.enter_context(nc.psum_tensor(f"s1_{i}", [P, 512], F32)) for i in range(S1N)]
        s2 = [ctx.enter_context(nc.psum_tensor(f"s2_{i}", [P, 512], F32)) for i in range(S2N)]
        pv = ctx.enter_context(nc.psum_tensor("pv", [P, 512], F32))
        misc = [ctx.enter_context(nc.psum_tensor(f"misc{i}", [P, 512], F32)) for i in range(MN)] + s1

        x_sb = sb("x_sb", [P, B, NB, C], F32)
        c_sb = sb("c_sb", [P, B, NB, C], F32)
        wqk = sb("wqk", [P, 4 * C], F32)
        wq, wk = wqk[:, 0:2 * C], wqk[:, 2 * C:4 * C]
        wvo = sb("wvo", [P, 2 * C], F32)
        wv, wo = wvo[:, 0:C], wvo[:, C:2 * C]
        small = sb("small", [P, 3 * C + 4 + 3], F32)
        ident, bvb, bob = (small[:, i * C:(i + 1) * C] for i in range(3))
        qkbias, sc = small[:, 3 * C:3 * C + 4], small[:, 3 * C + 4:3 * C + 7]
        identb = sb("identb", [P, P], BF16)
        sel = sb("sel", [FIRST * 2 * HD, NSEL, P], BF16)
        rot = sb("rot", [P, 4, T], F32)
        mask8 = sb("mask8", [B, T], U8)
        maskb = sb("maskb", [B, T], BF16)
        maskT = sb("maskT", [P, B, NB], U8)
        k0 = sb("k0", [P, 2, FH], U8)
        k1 = sb("k1", [P, KC, FH], U8)
        k2 = sb("k2", [P, KC, C], U8)
        sgn = sb("sgn", [P, 8], F32)
        w0d = sb("w0d", [P, 2, FH], F32)
        w0 = sb("w0", [P, FH], F16)
        w1 = sb("w1", [P, KC, FH], F16)
        w2 = sb("w2", [P, KC, C], F16)
        alpha = sb("alpha", [P, 4], F32)
        minus1 = sb("minus1", [P, 1], F32)
        half = sb("half", [P, NB * B], F32)

        st1 = sb("st1", [P, B * NB, 6], F32)
        mv1 = sb("mv1", [P, B * NB, 2], F32)
        ve1 = sb("ve1", [P, B * NB], F32)
        rs1 = sb("rs1", [P, B * NB], F32)
        xn = sb("xn", [P, B, NB, C], F32)
        xb = sb("xb", [P, B, NB, C], F32)
        xcT = sb("xcT", [P, B, 2, T], F32)
        rca = sb("rca", [P, B, 2, T], F32)
        rcb = sb("rcb", [P, B, 2, T], F32)
        rq, rr = rca, rcb
        parts = sb("parts", [P, B, 2, PARTS, T], BF16)
        warm = sb("warm", [P, 512], BF16)
        ones = sb("ones", [1, T], BF16)
        onesf = sb("onesf", [1, P], F32)
        qz = sb("qz", [P, 2, H, T], BF16)
        ks = sb("ks", [P, B, PAIRS, T], BF16)
        va = sb("va", [P, B, NB, H, VW], F32)
        pt = sb("pt", [P, PN, NB, T], F32)
        mx = sb("mx", [P, NG, NB, G], F32)
        mr = sb("mr", [P, NG, 2, NB, G], F32)
        mh = sb("mh", [P, NG, NB, G, PARTS], BF16)
        mT = sb("mT", [2 * PARTS, NG, 2, T], BF16)
        attU = sb("attU", [P, 2, GPB, T], F32)
        rden = sb("rden", [P, B, NB, H], F32)
        att = sb("att", [P, B, NB, C], F32)
        attT = sb("attT", [P, B, T], F32)
        x1 = sb("x1", [P, B, NB, C], F32)
        st2 = sb("st2", [P, B * NB, 6], F32)
        mv2 = sb("mv2", [P, B * NB, 2], F32)
        ve2 = sb("ve2", [P, B * NB], F32)
        rs2 = sb("rs2", [P, B * NB], F32)
        ln2 = sb("ln2", [P, B, NB, C], F32)
        lnh = sb("lnh", [P, 2, T], F16)
        lnl = sb("lnl", [P, 2, T], F16)
        r1h = sb("r1h", [P, 2, KC, T], F16)
        r1l = sb("r1l", [P, 2, KC, T], F16)
        r2h = sb("r2h", [P, 2, KC, T], F16)
        r2l = sb("r2l", [P, 2, KC, T], F16)
        o_sb = xn

        x_first, x_rest, c_first, c_rest = (sem(n) for n in ("x_first", "x_rest", "c_first", "c_rest"))
        x_in = [x_first] + [x_rest] * (B - 1)
        c_in = [c_first] + [c_rest] * (B - 1)
        sel_in = sem("sel_in")
        small_in, identb_in, wqk_in, wvo_in, rot_in = (
            sem(n) for n in ("small_in", "identb_in", "wqk_in", "wvo_in", "rot_in"))
        mask_in, maskT_in, k0_in, k1_in, k2_in = (sem(n) for n in ("mask_in", "maskT_in", "k0_in", "k1_in", "k2_in"))
        extra_out, mask_out, ones_in = sem("extra_out"), sem("mask_out"), sem("ones_in")
        parts_out = [sem(f"parts_out{b}") for b in range(B)]
        stack_in = [[sem(f"stack_in{b}_{c}") for c in range(len(LOADS[b]))] for b in range(B)]
        shift_in = [sem(f"shift_in{g}") for g in range(NG)]
        out_done = sem("out_done")
        misc_full = [sem(f"misc_full{i}") for i in range(MN + S1N)]
        names = ("half_set", "va_set", "keep_done", "warm_set", "qz_even_set", "qz_odd_set", "maskb_done",
                 "stats1", "aggr1", "var1", "rstd1", "xn_done", "xb_done",
                 "ones_set", "onesf_set", "stack_full", "first_k", "first_q", "xcT_done", "rc_done", "va_done",
                 "w0_step", "w0_done", "w1_done", "w2_done", "alpha_step",
                 "s1_full", "max_done", "m_step", "mparts_done", "mT_done", "s2_full", "exp_done",
                 "pv_full", "attU_done", "rden_done", "att_done", "attT_done", "x1_done", "stats2", "aggr2",
                 "var2", "rstd2", "ln2_done", "lnh_done", "lnl_done", "r1h_done", "r1l_done", "r2h_done",
                 "r2l_done", "o_done")
        S = {n: sem(n) for n in names}
        split_q0, split_k0 = sem("split_q0"), sem("split_k0")
        split_done = [(split_q0, split_k0)] + [(x, x) for x in (sem(f"split{b}") for b in range(1, B))]
        sm = lambda n: S[n]

        block = ctx.enter_context(nc.Block())

        @block.sync
        def _(sp):
            sp.dma_start(x_sb[:, 0], d["x"][0].rearrange("(n p) c -> p n c", p=P)).then_inc(x_first, 16)
            sp.dma_start(wqk[:], d["wqk"]).then_inc(wqk_in, 16)
            tail = "b (n p) c -> p (b n) c"
            sp.dma_start(x_sb[:, 1:].rearrange("p b n c -> p (b n) c"), d["x"][1:].rearrange(tail, p=P)).then_inc(x_rest, 16)
            sp.dma_start(rot[:], d["rot"]).then_inc(rot_in, 16)
            sp.dma_start(mask8[:], d["mask"]).then_inc(mask_in, 16)
            sp.dma_start(sel[:], d["sel"]).then_inc(sel_in, 16)
            sp.dma_start(d["scr"][:, :, :, EXTRA].rearrange("b i p t -> b (i p) t"),
                         d["extra"].unsqueeze(0).to_broadcast([B, 2 * P, T])).then_inc(extra_out, 16)
            sp.dma_start(wvo[:], d["wvo"]).then_inc(wvo_in, 16)
            sp.dma_start(c_sb[:, 1:].rearrange("p b n c -> p (b n) c"), d["ctx"][1:].rearrange(tail, p=P)).then_inc(c_rest, 16)
            sp.dma_start(identb[:], d["identb"]).then_inc(identb_in, 16)
            sp.dma_start(k0[:], d["k0"].rearrange("(i p) f -> p i f", p=P)).then_inc(k0_in, 16)
            sp.dma_start(maskT[:], d["maskT"]).then_inc(maskT_in, 16)
            sp.wait_ge(sm("maskb_done"), 1)
            sp.wait_ge(extra_out, 16)
            sp.dma_start(d["scr"][:, 1, :, EXTRA].rearrange("b (j e) t -> e b j t", e=2 * HD)[MASKF],
                         maskb[:].unsqueeze(1).to_broadcast([B, PAIRS, T])).then_inc(mask_out, 16)
            sp.wait_ge(sm("qz_odd_set"), 1)
            r = SLOTS * MASKF + EXTRA
            sp.dma_start(qz[r:r + 1].rearrange("p w (j e) t -> p (w j) e t", e=2)[:, :, 1],
                         d["extra"][MASKF:MASKF + 1].unsqueeze(1).to_broadcast([1, 2 * PAIRS, T])).then_inc(ones_in, 16)

            def split_part(i, b, part):
                sp.wait_ge(split_done[b][i], (2, 4, 5)[part])

            def store_parts(b):
                q, k = d["scr"][b, 0], d["scr"][b, 1]
                split_part(1, b, 0)
                sp.dma_start(k[:, 0:3], parts[:, b, 1, 0:1].to_broadcast([P, 3, T])).then_inc(parts_out[b], 16)
                split_part(0, b, 0)
                sp.dma_start(q[:, 6:7], parts[:, b, 0, 0:1]).then_inc(parts_out[b], 16)
                split_part(1, b, 1)
                sp.dma_start(k[:, 3:6], parts[:, b, 1, 1:2].to_broadcast([P, 3, T])).then_inc(parts_out[b], 16)
                split_part(1, b, 2)
                sp.dma_start(k[:, 6:7], parts[:, b, 1, 2:3]).then_inc(parts_out[b], 16)
                split_part(0, b, 2)
                sp.dma_start(q[:, 0:6].rearrange("p (m s) t -> p m (s t)", m=2),
                             parts[:, b, 0].rearrange("p s t -> p (s t)").unsqueeze(1).to_broadcast([P, 2, 3 * T]))\
                    .then_inc(parts_out[b], 16)

            def load_stacks(b, c):
                q, k = d["scr"][b, 0], d["scr"][b, 1]
                js = slice(LOADS[b][c], (LOADS[b] + (PAIRS,))[c + 1])
                if b == 0 and c == 0:
                    sp.wait_ge(mask_out, 16)
                    sp.wait_ge(sm("qz_even_set"), 1)
                    sp.wait_ge(sm("qz_odd_set"), 1)
                sp.wait_ge(parts_out[b], 5 * 16)
                sp.dma_start(ks[:, b, js], k.rearrange("(j e) s t -> (e s) j t", e=2 * HD)[:, js]).then_inc(stack_in[b][c], 16)
                if b >= 2:
                    sp.wait_ge(sm("s2_full"), H * (b - 2) + 2 * js.stop)
                for par in range(2):
                    r = SROWS * par
                    heads_ = slice(2 * js.start + par, 2 * js.stop, 2)
                    sp.dma_start(qz[r:r + SROWS, b % 2, heads_],
                                 q.rearrange("(j two e) s t -> two (e s) j t", two=2, e=HD)[par][:, js])\
                        .then_inc(stack_in[b][c], 16)

            def shift(g):
                b, h0 = divmod(G * g, H)
                sp.wait_ge(sm("mT_done"), g + 1)
                for par in range(2):
                    r = SROWS * par + EXTRA
                    sp.dma_start(qz[r:r + SLOTS * (PARTS - 1) + 1:SLOTS, b % 2, h0 + par:h0 + G:2],
                                 mT[PARTS * par:PARTS * (par + 1), g]).then_inc(shift_in[g], 16)

            def store(b):
                sp.wait_ge(sm("o_done"), b + 1)
                sp.dma_start(d["out"][b].rearrange("(n p) c -> p n c", p=P), o_sb[:, b]).then_inc(out_done, 16)

            for s in range(-1, last_step + 1):
                for kind, b in side.get(s, []):
                    if kind == "M":
                        shift(b)
                    if kind == "O":
                        store(b)
                for kind, b in side.get(s, []):
                    if kind == "Y":
                        store_parts(b)
                    if kind == "Z":
                        load_stacks(*b)
                    if kind == "Z" and b == (0, len(LOADS[0]) - 1):
                        sp.dma_start(k1[:], d["k1"].rearrange("(k p) f -> p k f", p=P)).then_inc(k1_in, 16)
                        sp.dma_start(k2[:], d["k2"].rearrange("(k p) f -> p k f", p=P)).then_inc(k2_in, 16)
            sp.wait_ge(out_done, 16 * B)

        def split(eng, b, i, step):
            done = split_done[b][i % 2]
            of = slice(0, 2) if i == 2 else slice(i, i + 1)
            r, rest = rq[:, b, of], rr[:, b, of]
            part = [parts[:, b, of, k] for k in range(PARTS)]
            copy = eng.copy if eng is nc.scalar else eng.tensor_copy if eng is nc.vector else None
            if step == 0:
                eng.wait_ge(sm("rc_done"), 4 * b + (4 if i == 2 else 2 * i + 2))
                ins = eng.tensor_tensor(r, rca[:, b, of], rcb[:, b, of], ALU.add)
            else:
                eng.wait_ge(done, step)
                if step == 1:
                    ins = copy(part[0], r)
                if step == 2:
                    ins = eng.tensor_tensor(rest, r, part[0], ALU.subtract)
                if step == 3:
                    ins = copy(part[1], rest)
                if step == 4:
                    ins = eng.tensor_tensor(part[2], rest, part[1], ALU.subtract)
            ins.then_inc(done, 1)

        @block.tensor
        def _(pe):
            def bank(task):
                k, _ = slot_of[task]
                return misc[k], misc_full[k]

            def claim(task):
                k, _ = slot_of[task]
                if before[task] == "maxima":
                    pe.wait_ge(sm("max_done"), heads)
                elif before[task]:
                    kind, b = before[task]
                    reader, count = {
                        "T": ("xcT_done", b + 1), "Q": ("rc_done", 4 * b + 2), "K": ("rc_done", 4 * b + 4),
                        "V": ("va_done", b + 1), "M": ("mT_done", b + 1),
                        "N1": ("att_done", NB * b + 1), "N1b": ("att_done", NB * b + 2),
                        "N2": ("attT_done", b + 1), "N3": ("x1_done", b + 1), "N4": ("lnl_done", b + 1),
                        "Fa": ("r1l_done", 2 * b + 1), "Fb": ("r1l_done", 2 * b + 2),
                        "Ga": ("r2l_done", 2 * b + 1), "Gb": ("r2l_done", 2 * b + 2), "O": ("o_done", b + 1),
                    }[kind]
                    pe.wait_ge(sm(reader), count)
                return misc[k], misc_full[k]

            def T_(b):
                pe.wait_ge(sm("xn_done"), b + 1)
                pe.wait_ge(c_in[b], 16)
                if b == 0:
                    pe.wait_ge(small_in, 16)
                ps, full = claim(("T", b))
                for n in range(NB):
                    pe.transpose(ps[:, n * P:(n + 1) * P], xn[:, b, n], ident[:])
                for n in range(NB):
                    mm = pe.transpose(ps[:, T + n * P:T + (n + 1) * P], c_sb[:, b, n], ident[:])
                mm.then_inc(full, 1)

            def QK_(b, kind):
                pe.wait_ge(sm("xcT_done"), b + 1)
                if b == 0 and kind == "Q":
                    pe.wait_ge(wqk_in, 16)
                ps, full = claim((kind, b))
                w, i = (wq, 0) if kind == "Q" else (wk, 1)
                for r in range(2):
                    mm = pe.matmul(ps[:, r * T:(r + 1) * T], w[:, r * C:(r + 1) * C], xcT[:, b, i], start=True, stop=True)
                mm.then_inc(full, 1)

            def V_(b):
                if b == 0:
                    pe.wait_ge(wvo_in, 16)
                    pe.wait_ge(sm("onesf_set"), 1)
                ps, full = claim(("V", b))
                for n in range(NB):
                    pe.matmul(ps[:, n * C:(n + 1) * C], xcT[:, b, 1, n * P:(n + 1) * P], wv[:], start=True, stop=False)
                    mm = pe.matmul(ps[:, n * C:(n + 1) * C], onesf[:], bvb[0:1], start=False, stop=True)
                mm.then_inc(full, 1)

            def M_(g):
                pe.wait_ge(sm("mparts_done"), g + 1)
                ps, full = claim(("M", g))
                out = ps[:].bitcast(BF16)
                if g == 0:
                    pe.wait_ge(identb_in, 16)
                for m in range(2):
                    for n in range(NB):
                        at_ = (m * NB + n) * P
                        mm = pe.transpose(out[0:2 * PARTS, at_:at_ + P],
                                          mh[:, g, n, 2 * m:2 * m + 2].rearrange("p g k -> p (g k)"), identb[:])
                mm.then_inc(full, 1)

            def first_stack(j):
                rows = slice(0, FIRST * 2 * HD)

                def select(ps, i, at_):
                    for k in range(PARTS):
                        if j == 0:
                            pe.wait_ge((split_q0, split_k0)[i], (2, 4, 5)[k])
                        pe.matmul(ps, sel[:, at_ + k], parts[rows, 0, i, k], start=(k == 0), stop=False)

                if j == 0:
                    pe.wait_ge(sel_in, 16)
                kps = (s1[0], s2[0])[j][:, 0:T]
                select(kps, 1, PARTS * j)
                if j == 0:
                    pe.wait_ge(sm("maskb_done"), 1)
                    pe.wait_ge(sm("ones_set"), 1)
                pe.matmul(kps, sel[0:B, NSEL - 2], maskb[:], start=False, stop=False)
                pe.matmul(kps, sel[0:1, NSEL - 1], ones[:], start=False, stop=True).then_inc(sm("stack_full"), 1)
                for par in range(2):
                    qps = (s2[1], pv)[j][:, par * T:(par + 1) * T]
                    select(qps, 0, PARTS * (FIRST + 2 * j + par))
                    mm = pe.matmul(qps, sel[0:1, NSEL - 2], ones[:], start=False, stop=True)
                mm.then_inc(sm("stack_full"), 1)

            def score_max(i):
                b, h = divmod(i, H)
                if i < 2 * FIRST and i % 2 == 0:
                    pe.wait_ge(sm("first_k"), i // 2 + 1)
                    pe.wait_ge(sm("first_q"), i // 2 + 1)
                if i == 2 * FIRST:
                    pe.wait_ge(ones_in, 16)
                if h % 2 == 0 and h // 2 in LOADS[b]:
                    pe.wait_ge(stack_in[b][LOADS[b].index(h // 2)], 3 * 16)
                if i >= S1N:
                    pe.wait_ge(sm("max_done"), i - S1N + 1)
                for n in range(NB):
                    mm = pe.matmul(s1[i % S1N][:, n * T:(n + 1) * T], qz[:, b % 2, h, n * P:(n + 1) * P],
                                   ks[:, b, h // 2], start=True, stop=True)
                mm.then_inc(sm("s1_full"), 1)

            def score_exp(i):
                b, h = divmod(i, H)
                if i % G == 0:
                    pe.wait_ge(shift_in[i // G], 2 * 16)
                if i >= S2N:
                    pe.wait_ge(sm("exp_done"), i - S2N + 1)
                for n in range(NB):
                    mm = pe.matmul(s2[i % S2N][:, n * T:(n + 1) * T], ks[:, b, h // 2, n * P:(n + 1) * P],
                                   qz[:, b % 2, h], start=True, stop=True)
                mm.then_inc(sm("s2_full"), 1)

            def values(g, n):
                b, h0 = divmod(G * g, H)
                if n == 0:
                    pe.wait_ge(sm("exp_done"), G * (g + 1))
                    pe.wait_ge(sm("va_done"), b + 1)
                    if g == 0:
                        pe.wait_ge(sm("va_set"), 1)
                        pe.wait_ge(sm("keep_done"), 1)
                    if g >= 1:
                        pe.wait_ge(sm("attU_done"), g)
                for j in range(G):
                    mm = pe.matmul(pv[VW * j:VW * (j + 1), 0:T], va[:, b, n, h0 + j],
                                   pt[:, (G * g + j) % PN, n], start=(n == 0), stop=(n == NB - 1))
                if n == NB - 1:
                    mm.then_inc(sm("pv_full"), 1)

            def N1_(b, n):
                pe.wait_ge(sm("attU_done"), GPB * (b + 1))
                ps, full = claim(("N1" if n == 0 else "N1b", b))
                for q in range(GPB):
                    mm = pe.transpose(ps[:, q * P:(q + 1) * P], attU[:, b % 2, q, n * P:(n + 1) * P], ident[:])
                mm.then_inc(full, 1)

            def N2_(b):
                ps, full = claim(("N2", b))
                for n in range(NB):
                    pe.wait_ge(sm("att_done"), NB * b + n + 1)
                    mm = pe.transpose(ps[:, n * P:(n + 1) * P], att[:, b, n], ident[:])
                mm.then_inc(full, 1)

            def N3_(b):
                pe.wait_ge(sm("attT_done"), b + 1)
                ps, full = claim(("N3", b))
                for n in range(NB):
                    mm = pe.matmul(ps[:, n * C:(n + 1) * C], attT[:, b, n * P:(n + 1) * P], wo[:], start=True, stop=True)
                mm.then_inc(full, 1)

            def N4_(b):
                ps, full = claim(("N4", b))
                for n in range(NB):
                    pe.wait_ge(sm("ln2_done"), NB * b + n + 1)
                    mm = pe.transpose(ps[:, n * P:(n + 1) * P], ln2[:, b, n], ident[:])
                mm.then_inc(full, 1)

            def F_(b, f):
                if b == 0 and f == 0:
                    pe.wait_ge(sm("w0_done"), 1)
                ps, full = claim(("Fa" if f == 0 else "Fb", b))
                for o in range(2):
                    w = w0[:, (2 * f + o) * P:(2 * f + o + 1) * P]
                    for part, done in ((lnh, "lnh_done"), (lnl, "lnl_done")):
                        pe.wait_ge(sm(done), b + 1)
                        mm = pe.matmul(ps[:, o * T:(o + 1) * T], w, part[:, b % 2], start=part is lnh, stop=part is lnl)
                mm.then_inc(full, 1)

            def G_(b, f, o):
                kind = ("Ga", "Gb")[f]
                if b == 0 and f == 0 and o == 0:
                    pe.wait_ge(sm("w1_done"), KC)
                ps, full = claim((kind, b)) if o == 0 else bank((kind, b))
                for part, done in ((r1h, "r1h_done"), (r1l, "r1l_done")):
                    for k in range(KC):
                        pe.wait_ge(sm(done), 2 * b + k // 2 + 1)
                        mm = pe.matmul(ps[:, o * T:(o + 1) * T], w1[:, k, (2 * f + o) * P:(2 * f + o + 1) * P],
                                       part[:, b % 2, k], start=(part is r1h and k == 0),
                                       stop=(part is r1l and k == KC - 1))
                if o == 1:
                    mm.then_inc(full, 1)

            def O_(b):
                if b == 0:
                    pe.wait_ge(sm("w2_done"), 1)
                ps, full = claim(("O", b))
                for n in range(NB):
                    for part, done in ((r2h, "r2h_done"), (r2l, "r2l_done")):
                        for k in range(KC):
                            pe.wait_ge(sm(done), 2 * b + k // 2 + 1)
                            mm = pe.matmul(ps[:, n * C:(n + 1) * C], part[:, b % 2, k, n * P:(n + 1) * P], w2[:, k],
                                           start=(part is r2h and k == 0), stop=(part is r2l and k == KC - 1))
                mm.then_inc(full, 1)

            tasks = {"T": T_, "Q": lambda b: QK_(b, "Q"), "K": lambda b: QK_(b, "K"), "V": V_, "M": M_,
                     "N1": lambda b: N1_(b, 0), "N1b": lambda b: N1_(b, 1), "N2": N2_, "N3": N3_, "N4": N4_,
                     "Fa": lambda b: F_(b, 0), "Fb": lambda b: F_(b, 1), "Ga": lambda b: G_(b, 0, 0),
                     "Ga2": lambda b: G_(b, 0, 1), "Gb": lambda b: G_(b, 1, 0), "Gb2": lambda b: G_(b, 1, 1), "O": O_}
            pe.wait_ge(sm("warm_set"), 1)
            for _ in range(WARM):
                pe.matmul(s1[0][:], warm[:, 0:P], warm[:], start=True, stop=True)
            for kind, b in tasks_at("pe", -1):
                if kind in tasks:
                    tasks[kind](b)
            for _ in range(WARM2):
                pe.matmul(s1[0][:], warm[:, 0:P], warm[:], start=True, stop=True)
            for j in range(FIRST):
                first_stack(j)
            for s in range(last_step + 1):
                if s < heads:
                    score_max(s)
                if s in exp_at:
                    score_exp(exp_at[s])
                for n in range(NB):
                    e = exp_at.get(s - PVLAG - n, 0)
                    if e % G == G - 1:
                        values(e // G, n)
                for kind, b in tasks_at("pe", s):
                    if kind in tasks:
                        tasks[kind](b)

        @block.vector
        def _(v):
            def open_(task):
                k, use = slot_of[task]
                v.wait_ge(misc_full[k], use + 1)
                return misc[k]

            def norm1(b):
                v.wait_ge(x_in[b], 16)
                for n in range(NB):
                    v.bn_stats(st1[:, b * NB + n], x_sb[:, b, n]).then_inc(sm("stats1"), 1)
                v.wait_ge(sm("stats1"), NB * (b + 1))
                for n in range(NB):
                    v.bn_aggr(mv1[:, b * NB + n], st1[:, b * NB + n]).then_inc(sm("aggr1"), 1)

            def norm1b(b):
                v.wait_ge(sm("rstd1"), b + 1)
                for n in range(NB):
                    i = b * NB + n
                    ins = v.tensor_scalar(xn[:, b, n], x_sb[:, b, n], mv1[:, i, 0:1], rs1[:, i:i + 1], ALU.subtract, ALU.mult)
                ins.then_inc(sm("xn_done"), 1)

            def rope(b, kind):
                i = 0 if kind == "Q" else 1
                if b == 0 and i == 0:
                    v.wait_ge(rot_in, 16)
                    v.wait_ge(small_in, 16)
                ps = open_((kind, b))
                v.scalar_tensor_tensor(rca[:, b, i], ps[:, 0:T], qkbias[:, 2 * i:2 * i + 1], rot[:, 2 * i], ALU.add, ALU.mult)\
                    .then_inc(sm("rc_done"), 1)
                v.scalar_tensor_tensor(rcb[:, b, i], ps[:, T:2 * T], qkbias[:, 2 * i + 1:2 * i + 2], rot[:, 2 * i + 1],
                                       ALU.add, ALU.mult).then_inc(sm("rc_done"), 1)

            def maximum(i):
                g, j = divmod(i, G)
                v.wait_ge(sm("s1_full"), i + 1)
                v.tensor_reduce(mx[:, g, :, j], s1[i % S1N][:].rearrange("p (n t) -> p n t", n=NB), AX.X, ALU.max)\
                    .then_inc(sm("max_done"), 1)

            def N1_(b, n):
                ps = open_(("N1" if n == 0 else "N1b", b))
                heads_ = ps[:].rearrange("p (h w) -> p h w", w=VW)
                v.reciprocal(rden[:, b, n], heads_[:, :, HD]).then_inc(sm("rden_done"), 1)
                v.wait_ge(sm("rden_done"), NB * b + n + 1)
                v.tensor_tensor(att[:, b, n].rearrange("p (h e) -> p h e", h=H), heads_[:, :, 0:HD],
                                rden[:, b, n].unsqueeze(2).to_broadcast([P, H, HD]), ALU.mult).then_inc(sm("att_done"), 1)

            def N3_(b):
                ps = open_(("N3", b))
                v.wait_ge(sm("xb_done"), b + 1)
                v.tensor_tensor(x1[:, b].rearrange("p n c -> p (n c)"), ps[:, 0:NB * C], xb[:, b].rearrange("p n c -> p (n c)"),
                                ALU.add).then_inc(sm("x1_done"), 1)
                v.wait_ge(sm("x1_done"), b + 1)
                for n in range(NB):
                    v.bn_stats(st2[:, b * NB + n], x1[:, b, n]).then_inc(sm("stats2"), 1)
                v.wait_ge(sm("stats2"), NB * (b + 1))
                for n in range(NB):
                    v.bn_aggr(mv2[:, b * NB + n], st2[:, b * NB + n]).then_inc(sm("aggr2"), 1)

            def N3b_(b):
                v.wait_ge(sm("rstd2"), b + 1)
                for n in range(NB):
                    i = b * NB + n
                    v.tensor_scalar(ln2[:, b, n], x1[:, b, n], mv2[:, i, 0:1], rs2[:, i:i + 1], ALU.subtract, ALU.mult)\
                        .then_inc(sm("ln2_done"), 1)

            def N4_(b):
                ps = open_(("N4", b))
                v.wait_ge(sm("lnh_done"), b + 1)
                v.scalar_tensor_tensor(lnl[:, b % 2], ps[:, 0:T], LNS, lnh[:, b % 2], ALU.mult, ALU.subtract).then_inc(sm("lnl_done"), 1)

            def relu_lo(b, f, kinds, hi, lo, hi_done, lo_done):
                ps = open_((kinds[f], b))
                v.wait_ge(sm(hi_done), 2 * b + f + 1)
                v.scalar_tensor_tensor(lo[:, b % 2, 2 * f:2 * f + 2].rearrange("p k t -> p (k t)"), ps[:], 0.0,
                                       hi[:, b % 2, 2 * f:2 * f + 2].rearrange("p k t -> p (k t)"), ALU.max, ALU.subtract)\
                    .then_inc(sm(lo_done), 1)

            def O_(b):
                ps = open_(("O", b))
                if b == 0:
                    v.wait_ge(sm("alpha_step"), 3)
                v.scalar_tensor_tensor(o_sb[:, b].rearrange("p n c -> p (n c)"), ps[:, 0:NB * C], alpha[:, 2:3],
                                       x1[:, b].rearrange("p n c -> p (n c)"), ALU.mult, ALU.add).then_inc(sm("o_done"), 1)

            def first_k(j):
                v.wait_ge(sm("stack_full"), 2 * j + 1)
                v.tensor_copy(ks[:, 0, j], (s1[0], s2[0])[j][:, 0:T]).then_inc(sm("first_k"), 1)

            tasks = {"L": norm1, "Lx": norm1b, "Q": lambda b: rope(b, "Q"), "K": lambda b: rope(b, "K"), 
                     "N1": lambda b: N1_(b, 0), "N1b": lambda b: N1_(b, 1), "N3": N3_, "N3x": N3b_, "N4": N4_,
                     "Fa": lambda b: relu_lo(b, 0, ("Fa", "Fb"), r1h, r1l, "r1h_done", "r1l_done"),
                     "Fb": lambda b: relu_lo(b, 1, ("Fa", "Fb"), r1h, r1l, "r1h_done", "r1l_done"),
                     "Ga2": lambda b: relu_lo(b, 0, ("Ga", "Gb"), r2h, r2l, "r2h_done", "r2l_done"),
                     "Gb2": lambda b: relu_lo(b, 1, ("Ga", "Gb"), r2h, r2l, "r2h_done", "r2l_done"), "O": O_}

            v.memset(qz[SROWS:P, :, 0::2, :].bitcast(mybir.dt.uint32), 0).then_inc(sm("qz_even_set"), 1)
            norm1(0)
            norm1b(0)
            v.wait_ge(mask_in, 16)
            v.tensor_scalar(maskb[:], mask8[:], -3.0e38, None, ALU.mult).then_inc(sm("maskb_done"), 1)
            norm1(1)
            rope(0, "Q")
            rope(0, "K")
            for step in range(5):
                split(nc.vector, 0, 1, step)
            norm1b(1)
            first_k(0)
            first_k(1)
            for s in range(last_step + 1):
                if s < heads:
                    maximum(s)
                for kind, b in tasks_at("dve", s):
                    if kind in tasks:
                        tasks[kind](b)

        @block.scalar
        def _(a):
            a.dma_start(small[:], d["small"]).then_inc(small_in, 16)
            a.dma_start(c_sb[:, 0], d["ctx"][0].rearrange("(n p) c -> p n c", p=P)).then_inc(c_first, 16)

            def open_(task):
                k, use = slot_of[task]
                a.wait_ge(misc_full[k], use + 1)
                return misc[k]

            def T_(b):
                ps = open_(("T", b))
                a.copy(xcT[:, b].rearrange("p i t -> p (i t)"), ps[:]).then_inc(sm("xcT_done"), 1)

            def V_(b):
                ps = open_(("V", b))
                a.copy(va[:, b, :, :, 0:HD].rearrange("p n h e -> p (n h) e"),
                       ps[:, 0:NB * C].rearrange("p (h e) -> p h e", e=HD)).then_inc(sm("va_done"), 1)

            def M_(g):
                ps = open_(("M", g))
                a.copy(mT[:, g].rearrange("p m t -> p (m t)"), ps[:].bitcast(BF16)[0:2 * PARTS, 0:2 * T]).then_inc(sm("mT_done"), 1)

            def exponential(i):
                a.wait_ge(sm("s2_full"), i + 1)
                if i >= PN:
                    a.wait_ge(sm("pv_full"), (i - PN) // G + 1)
                a.activation(pt[:, i % PN].rearrange("p n t -> p (n t)"), s2[i % S2N][:], ACT.Exp).then_inc(sm("exp_done"), 1)

            def attU_copy(g):
                b = g // GPB
                if b >= 2 and g % GPB == 0:
                    a.wait_ge(sm("att_done"), NB * (b - 1))
                a.wait_ge(sm("pv_full"), g + 1)
                a.copy(attU[:, b % 2, g % GPB], pv[:, 0:T]).then_inc(sm("attU_done"), 1)

            def N2_(b):
                ps = open_(("N2", b))
                a.copy(attT[:, b], ps[:, 0:T]).then_inc(sm("attT_done"), 1)

            def N4_(b):
                ps = open_(("N4", b))
                if b >= 2:
                    a.wait_ge(sm("r1h_done"), 2 * (b - 1))
                a.activation(lnh[:, b % 2], ps[:, 0:T], ACT.Copy, scale=LNS).then_inc(sm("lnh_done"), 1)

            def relu_hi(b, f, kinds, hi, hi_done):
                ps = open_((kinds[f], b))
                a.activation(hi[:, b % 2, 2 * f:2 * f + 2].rearrange("p k t -> p (k t)"), ps[:], ACT.Relu)\
                    .then_inc(sm(hi_done), 1)

            def w12(k):
                if k == 0:
                    a.wait_ge(k1_in, 16)
                    a.wait_ge(sm("w0_step"), 5)
                if k < KC:
                    a.activation(w1[:, k], k1[:, k], ACT.Identity, bias=sgn[:, 7:8], scale=sgn[:, 6:7]).then_inc(sm("w1_done"), 1)
                else:
                    a.wait_ge(k2_in, 16)
                    a.wait_ge(sm("half_set"), 2)
                    a.activation(w2[:].rearrange("p k c -> p (k c)"), k2[:].rearrange("p k c -> p (k c)"), ACT.Identity,
                                 bias=minus1[:], scale=2.0).then_inc(sm("w2_done"), 1)

            tasks = {"V": V_, "w1": w12, "w2": w12, "X1": lambda b: split(nc.scalar, b, 2, 1), "X3": lambda b: split(nc.scalar, b, 2, 3), "T": T_, "M": M_, "N2": N2_, "N4": N4_,
                     "Fa": lambda b: relu_hi(b, 0, ("Fa", "Fb"), r1h, "r1h_done"),
                     "Fb": lambda b: relu_hi(b, 1, ("Fa", "Fb"), r1h, "r1h_done"),
                     "Ga2": lambda b: relu_hi(b, 0, ("Ga", "Gb"), r2h, "r2h_done"),
                     "Gb2": lambda b: relu_hi(b, 1, ("Ga", "Gb"), r2h, "r2h_done")}
            def first_q(j):
                a.wait_ge(sm("stack_full"), 2 * j + 2)
                if j == 0:
                    a.wait_ge(ones_in, 16)
                    a.wait_ge(sm("qz_even_set"), 1)
                a.copy(qz[:, 0, 2 * j:2 * j + 2].rearrange("p h t -> p (h t)"), (s2[1], pv)[j][:]).then_inc(sm("first_q"), 1)

            T_(0)
            split(nc.scalar, 0, 0, 1)
            split(nc.scalar, 0, 0, 3)
            V_(0)
            for j in range(FIRST):
                first_q(j)
            for s in range(last_step + 1):
                if s in exp_at:
                    exponential(exp_at[s])
                e = exp_at.get(s - PVLAG - 1, 0)
                if e % G == G - 1:
                    attU_copy(e // G)
                for kind, b in tasks_at("act", s):
                    if kind in tasks:
                        tasks[kind](b)

        @block.gpsimd
        def _(p):
            p.memset(warm[:], 0.0).then_inc(sm("warm_set"), 1)
            p.memset(onesf[:], 1.0).then_inc(sm("onesf_set"), 1)
            p.memset(ones[:], 1.0).then_inc(sm("ones_set"), 1)
            p.memset(half[:], -0.5).then_inc(sm("half_set"), 1)
            p.memset(minus1[:], -1.0).then_inc(sm("half_set"), 1)
            p.memset(qz[0:SROWS, :, 1::2, :].bitcast(mybir.dt.uint32), 0).then_inc(sm("qz_odd_set"), 1)

            def rstd(b, mv, ve, out, aggr, var):
                cols = slice(NB * b, NB * (b + 1))
                p.wait_ge(sm(aggr), NB * (b + 1))
                p.tensor_scalar(ve[:, cols], mv[:, cols, 1], EPS, None, ALU.add).then_inc(sm(var), 1)
                p.wait_ge(sm(var), b + 1)
                return p.tensor_tensor(out, ve[:, cols], half[:, cols], ALU.pow)

            p.wait_ge(sm("half_set"), 1)
            def norm1(b):
                rstd(b, mv1, ve1, rs1[:, NB * b:NB * (b + 1)], "aggr1", "var1").then_inc(sm("rstd1"), 1)

            norm1(0)
            p.memset(va[:, :, :, :, HD + 1:VW], 0.0).then_inc(sm("va_set"), 1)
            norm1(1)
            split(nc.gpsimd, 0, 0, 0)
            split(nc.gpsimd, 0, 0, 2)
            split(nc.gpsimd, 0, 0, 4)
            p.wait_ge(small_in, 16)
            n = 0

            def step(ins):
                nonlocal n
                n += 1
                ins.then_inc(sm("w0_step"), 1)
                p.wait_ge(sm("w0_step"), n)

            step(p.tensor_scalar(sgn[:, 0:2], sc[:, 0:2], 0.0, 2.0, ALU.is_ge, ALU.mult))
            step(p.tensor_scalar(sgn[:, 2:4], sgn[:, 0:2], -1.0, None, ALU.add))
            step(p.tensor_tensor(sgn[:, 4:6], sgn[:, 2:4], sc[:, 0:2], ALU.mult))
            step(p.tensor_scalar(sgn[:, 6:7], sgn[:, 3:4], 2 * S1S, None, ALU.mult))
            step(p.tensor_scalar(sgn[:, 7:8], sgn[:, 3:4], -S1S, None, ALU.mult))
            p.tensor_tensor(alpha[:, 0:1], sgn[:, 4:5], sgn[:, 5:6], ALU.mult).then_inc(sm("alpha_step"), 1)
            p.wait_ge(sm("alpha_step"), 1)
            p.tensor_tensor(alpha[:, 1:2], alpha[:, 0:1], sc[:, 2:3], ALU.mult).then_inc(sm("alpha_step"), 1)
            p.wait_ge(sm("alpha_step"), 2)
            p.tensor_scalar(alpha[:, 2:3], alpha[:, 1:2], OUTS, None, ALU.mult).then_inc(sm("alpha_step"), 1)
            p.wait_ge(k0_in, 16)
            step(p.tensor_scalar(w0d[:], k0[:], sgn[:, 2:3], 2 * S0S, ALU.mult, ALU.mult))
            p.tensor_tensor(w0[:], w0d[:, 0], w0d[:, 1], ALU.subtract).then_inc(sm("w0_done"), 1)

            def xb_(b):
                p.wait_ge(x_in[b], 16)
                for n_ in range(NB):
                    ins = p.tensor_tensor(xb[:, b, n_], x_sb[:, b, n_], bob[:], ALU.add)
                ins.then_inc(sm("xb_done"), 1)

            def shift_parts(g):
                p.wait_ge(sm("max_done"), G * (g + 1))
                out = [mh[:, g, :, :, k] for k in range(PARTS)]
                p.tensor_scalar(out[0], mx[:, g], -1.0, None, ALU.mult).then_inc(sm("m_step"), 1)
                p.wait_ge(sm("m_step"), 4 * g + 1)
                p.tensor_tensor(mr[:, g, 0], mx[:, g], out[0], ALU.add).then_inc(sm("m_step"), 1)
                p.wait_ge(sm("m_step"), 4 * g + 2)
                p.tensor_scalar(out[1], mr[:, g, 0], -1.0, None, ALU.mult).then_inc(sm("m_step"), 1)
                p.wait_ge(sm("m_step"), 4 * g + 3)
                p.tensor_tensor(mr[:, g, 1], mr[:, g, 0], out[1], ALU.add).then_inc(sm("m_step"), 1)
                p.wait_ge(sm("m_step"), 4 * g + 4)
                p.tensor_scalar(out[2], mr[:, g, 1], -1.0, None, ALU.mult).then_inc(sm("mparts_done"), 1)

            def keep_column():
                p.wait_ge(maskT_in, 16)
                p.tensor_scalar(va[:, :, :, :, HD].rearrange("p b n h -> p (b n) h"),
                                maskT[:].rearrange("p b n -> p (b n)").unsqueeze(2).to_broadcast([P, B * NB, H]),
                                -1.0, 1.0, ALU.mult, ALU.add).then_inc(sm("keep_done"), 1)

            def N3_(b):
                cols = slice(b * NB, (b + 1) * NB)
                rstd(b, mv2, ve2, rs2[:, cols], "aggr2", "var2").then_inc(sm("rstd2"), 1)

            for s in range(last_step + 1):
                if s % G == G - 1 and s < heads:
                    shift_parts(s // G)
                for kind, b in tasks_at("pool", s):
                    if kind in ("X0", "X2", "X4"):
                        split(nc.gpsimd, b, 2, int(kind[1]))
                    if kind == "L":
                        norm1(b)
                    if kind == "keep":
                        keep_column()
                    if kind == "xb":
                        xb_(b)
                    if kind == "N3":
                        N3_(b)


def rotation_tables():
    f = np.float32
    scale_vec = (np.arange(0, HD, 2, dtype=f) + f(0.4 * HD)) / f(1.4 * HD)
    power = np.arange(-T // 2, -T // 2 + T, dtype=f) / f(64)
    scale = (scale_vec[None, :] ** power[:, None]).astype(f)
    inv_freq = (1.0 / f(10000.0) ** (np.arange(HD // 2, dtype=f) / f(HD // 2))).astype(f)
    ang = np.arange(T, dtype=f)[:, None] * inv_freq[None, :]
    sin, cos = np.sin(ang), np.cos(ang)
    sign = np.where(np.arange(HD) % 2 == 0, f(-1), f(1))
    rows = []
    for sc, by in ((scale, f(HD ** -0.5)), (f(1) / scale, f(1))):
        rows.append(np.repeat(cos * sc, 2, axis=1).T * by)
        rows.append(np.repeat(sin * sc, 2, axis=1).T * sign[:, None] * by)
    table = np.stack([np.tile(r, (H, 1)) for r in rows], axis=1)
    return np.ascontiguousarray(table.astype(f))


def selections():
    s = np.zeros((FIRST * 2, HD, NSEL, 2, HD, SLOTS), np.float32)
    for j in range(FIRST):
        for par in range(2):
            for e in range(HD):
                for slot in range(EXTRA):
                    s[2 * j + par, e, PARTS * j + KPART[slot], par, e, slot] = 1
                    s[2 * j + par, e, PARTS * (FIRST + 2 * j + par) + QPART[slot], par, e, slot] = 1
    s[0, 0, NSEL - 2, 0, MASKF, EXTRA] = 1
    s[0, 0, NSEL - 1, :, :PARTS, EXTRA] = 1
    return s.reshape(FIRST * 2 * HD, NSEL, P)


def kernel(**inputs):
    import concourse.bacc as bacc
    import ml_dtypes
    from concourse.bass_utils import run_bass_kernel_spmd

    g = {k: np.asarray(v) for k, v in inputs.items()}
    swap = np.arange(C).reshape(-1, 2)[:, ::-1].reshape(-1)
    wq, wk, bq, bk = (g[f"L0_xattn_{n}"] for n in ("Wq", "Wk", "bq", "bk"))
    extra = np.zeros((2, H, HD, T), np.float32)
    extra[0, :, MASKF] = 1
    extra[1, :, :PARTS] = 1
    extra = extra.reshape(2 * P, T)
    arrays = {
        "x": g["x"], "ctx": g["ctx_1024"], "mask": g["mask_BxS2_bf0"],
        "maskT": g["mask_BxS2_bf0"].reshape(B, NB, P).transpose(2, 0, 1),
        "wqk": np.concatenate([wq, wq[:, swap], wk, wk[:, swap]], axis=1),
        "wvo": np.concatenate([g["L0_xattn_Wv"], g["L0_xattn_Wo"]], axis=1),
        "small": np.concatenate([
            np.eye(P, dtype=np.float32), np.broadcast_to(g["L0_xattn_bv"], (P, C)),
            np.broadcast_to(g["L0_xattn_bo"], (P, C)), np.stack([bq, bq[swap], bk, bk[swap]], axis=1),
            np.broadcast_to(np.stack([g["L0_ffn_s0"], g["L0_ffn_s1"], g["L0_ffn_s2"]]), (P, 3))], axis=1),
        "k0": g["L0_ffn_k0"], "k1": g["L0_ffn_k1"], "k2": g["L0_ffn_k2"],
        "identb": np.eye(P).astype(ml_dtypes.bfloat16), "extra": extra.astype(ml_dtypes.bfloat16),
        "rot": rotation_tables(), "sel": selections().astype(ml_dtypes.bfloat16),
    }
    arrays = {k: np.ascontiguousarray(v) for k, v in arrays.items()}
    nc = bacc.Bacc("TRN2", target_bir_lowering=False, num_devices=1)
    d = {k: nc.dram_tensor(f"in_{k}", v.shape, mybir.dt.from_np(v.dtype), kind="ExternalInput").ap()
         for k, v in arrays.items()}
    d["scr"] = nc.dram_tensor("scr", (B, 2, P, SLOTS, T), BF16, kind="Internal").ap()
    d["out"] = nc.dram_tensor("out", (B, T, C), F32, kind="ExternalOutput").ap()
    program(nc, d)
    r = run_bass_kernel_spmd(nc, [{f"in_{k}": v for k, v in arrays.items()}], core_ids=[0])
    return r.results[0]["out"]
```
